# Optimizing a Trainium2 kernel written in Bass

```python
import numpy as np
import jax
import jax.numpy as jnp

def _softmax(x, axis=-1):
    return jax.nn.softmax(x, axis=axis)
def _gelu(x):
    return jax.nn.gelu(x, approximate=True)
def _silu(x):
    return jax.nn.silu(x)
def _sigmoid(x):
    return jax.nn.sigmoid(x)
def _layernorm(x, axis=-1, eps=1e-5):
    m = jnp.mean(x, axis=axis, keepdims=True)
    v = jnp.var(x, axis=axis, keepdims=True)
    return (x - m) / jnp.sqrt(v + eps)
def _scatter_add(tgt, idx, src, axis=0):
    return tgt.at[idx].add(src)
def _segment_sum(src, seg, n):
    return jax.ops.segment_sum(src, seg, n)

kernel_name = 'mk_conv_preact_d2_conv_nchw512_9f81dd'

def setup_inputs(seed: int = 0):
    np.random.seed(seed)
    _w = jnp.asarray
    def _rec_inputs():
        import jax
        import jax.numpy as jnp
        _gk = jax.random.key(seed)
        x = -0.0003929 + 0.9999 * jax.random.normal(jax.random.fold_in(_gk, 1), (8, 512, 64, 64), jnp.float32)
        return x
    x = _rec_inputs()
    def _L0_conv_setup():
        import jax, jax.numpy as jnp
        import numpy as np
        import math
        B, C, H, W, S = (8, 512, 64, 64, 4)
        key = jax.random.key(seed)
        ks = jax.random.split(key, 7)
        s = 1.0 / math.sqrt(C)
        x = jax.random.normal(ks[0], (B, C, H, W), jnp.float32)
        Wq = jax.random.uniform(ks[1], (C, C), jnp.float32, -s, s)
        bq = jax.random.uniform(ks[2], (C,), jnp.float32, -s, s)
        Wk = jax.random.uniform(ks[3], (C, C), jnp.float32, -s, s)
        bk = jax.random.uniform(ks[4], (C,), jnp.float32, -s, s)
        Wv = jax.random.uniform(ks[5], (C, C), jnp.float32, -s, s)
        bv = jax.random.uniform(ks[6], (C,), jnp.float32, -s, s)
        return {'x': x, 'Wq': Wq, 'bq': bq, 'Wk': Wk, 'bk': bk, 'Wv': Wv, 'bv': bv}
    _L0_conv_all = _L0_conv_setup()
    _L0_conv_in = {k: v for k, v in _L0_conv_all.items() if k in ('Wq', 'bq', 'Wk', 'bk', 'Wv', 'bv', )}
    del _L0_conv_all

    def _L1_conv_setup():
        import jax, jax.numpy as jnp
        from jax import lax
        import numpy as np
        INPUT_DIM = 512
        OUTPUT_DIM = 512
        D_STATE = 16
        D_CONV = 4
        EXPAND = 2
        D_MODEL = INPUT_DIM // 4
        D_INNER = EXPAND * D_MODEL
        DT_RANK = (D_MODEL + 15) // 16
        EPS = 1e-05

        def layer_norm(x, g, b):
            mu = jnp.mean(x, axis=-1, keepdims=True)
            var = jnp.mean((x - mu) ** 2, axis=-1, keepdims=True)
            return (x - mu) * lax.rsqrt(var + EPS) * g + b

        def mamba(x, in_proj_w, conv_w, conv_b, x_proj_w, dt_proj_w, dt_proj_b, A_log, D_param, out_proj_w):
            Beff, L, _ = x.shape
            xz = jnp.einsum('bld,ed->ble', x, in_proj_w)
            xi, z = jnp.split(xz, 2, axis=-1)
            xc = lax.conv_general_dilated(xi.transpose(0, 2, 1), conv_w[:, None, :], (1,), [(D_CONV - 1, 0)], feature_group_count=D_INNER)
            xc = jax.nn.silu(xc + conv_b[None, :, None]).transpose(0, 2, 1)
            dbc = jnp.einsum('bld,ed->ble', xc, x_proj_w)
            dt = dbc[..., :DT_RANK]
            Bs = dbc[..., DT_RANK:DT_RANK + D_STATE]
            Cs = dbc[..., DT_RANK + D_STATE:]
            dt = jax.nn.softplus(jnp.einsum('blr,er->ble', dt, dt_proj_w) + dt_proj_b)
            A = -jnp.exp(A_log)

            def step(h, inp):
                dt_t, B_t, C_t, x_t = inp
                dA = jnp.exp(dt_t[:, :, None] * A)
                h = dA * h + (dt_t * x_t)[:, :, None] * B_t[:, None, :]
                y = jnp.einsum('bds,bs->bd', h, C_t)
                return (h, y)
            h0 = jnp.zeros((Beff, D_INNER, D_STATE), x.dtype)
            _, ys = lax.scan(step, h0, (dt.transpose(1, 0, 2), Bs.transpose(1, 0, 2), Cs.transpose(1, 0, 2), xc.transpose(1, 0, 2)))
            y = ys.transpose(1, 0, 2) + xc * D_param
            y = y * jax.nn.silu(z)
            return jnp.einsum('bld,od->blo', y, out_proj_w)
        key = jax.random.key(seed)
        ks = jax.random.split(key, 10)
        inp = {'x': jax.random.normal(ks[0], (4, INPUT_DIM, 64, 64), jnp.float32), 'norm_g': jnp.ones((INPUT_DIM,), jnp.float32), 'norm_b': jnp.zeros((INPUT_DIM,), jnp.float32), 'in_proj_w': jax.random.normal(ks[1], (2 * D_INNER, D_MODEL), jnp.float32) * 0.02, 'conv_w': jax.random.normal(ks[2], (D_INNER, D_CONV), jnp.float32) * 0.2, 'conv_b': jnp.zeros((D_INNER,), jnp.float32), 'x_proj_w': jax.random.normal(ks[3], (DT_RANK + 2 * D_STATE, D_INNER), jnp.float32) * 0.02, 'dt_proj_w': jax.random.normal(ks[4], (D_INNER, DT_RANK), jnp.float32) * 0.1, 'dt_proj_b': jnp.full((D_INNER,), -2.0, jnp.float32), 'A_log': jnp.log(jnp.broadcast_to(jnp.arange(1, D_STATE + 1, dtype=jnp.float32), (D_INNER, D_STATE))), 'D_param': jnp.ones((D_INNER,), jnp.float32), 'out_proj_w': jax.random.normal(ks[5], (D_MODEL, D_INNER), jnp.float32) * 0.02, 'proj_w': jax.random.normal(ks[6], (OUTPUT_DIM, INPUT_DIM), jnp.float32) * 0.02, 'proj_b': jnp.zeros((OUTPUT_DIM,), jnp.float32), 'skip_scale': jnp.ones((1,), jnp.float32)}
        return inp
    _L1_conv_all = _L1_conv_setup()
    _L1_conv_in = {k: v for k, v in _L1_conv_all.items() if k in ('norm_g', 'norm_b', 'in_proj_w', 'conv_w', 'conv_b', 'x_proj_w', 'dt_proj_w', 'dt_proj_b', 'A_log', 'D_param', 'out_proj_w', 'proj_w', 'proj_b', 'skip_scale', )}
    del _L1_conv_all

    return {
        "x": x,
        "L0_conv_Wq": _L0_conv_in["Wq"],
        "L0_conv_bq": _L0_conv_in["bq"],
        "L0_conv_Wk": _L0_conv_in["Wk"],
        "L0_conv_bk": _L0_conv_in["bk"],
        "L0_conv_Wv": _L0_conv_in["Wv"],
        "L0_conv_bv": _L0_conv_in["bv"],
        "L1_conv_norm_g": _L1_conv_in["norm_g"],
        "L1_conv_norm_b": _L1_conv_in["norm_b"],
        "L1_conv_in_proj_w": _L1_conv_in["in_proj_w"],
        "L1_conv_conv_w": _L1_conv_in["conv_w"],
        "L1_conv_conv_b": _L1_conv_in["conv_b"],
        "L1_conv_x_proj_w": _L1_conv_in["x_proj_w"],
        "L1_conv_dt_proj_w": _L1_conv_in["dt_proj_w"],
        "L1_conv_dt_proj_b": _L1_conv_in["dt_proj_b"],
        "L1_conv_A_log": _L1_conv_in["A_log"],
        "L1_conv_D_param": _L1_conv_in["D_param"],
        "L1_conv_out_proj_w": _L1_conv_in["out_proj_w"],
        "L1_conv_proj_w": _L1_conv_in["proj_w"],
        "L1_conv_proj_b": _L1_conv_in["proj_b"],
        "L1_conv_skip_scale": _L1_conv_in["skip_scale"],
    }

def reference(x, L0_conv_Wq, L0_conv_bq, L0_conv_Wk, L0_conv_bk, L0_conv_Wv, L0_conv_bv, L1_conv_norm_g, L1_conv_norm_b, L1_conv_in_proj_w, L1_conv_conv_w, L1_conv_conv_b, L1_conv_x_proj_w, L1_conv_dt_proj_w, L1_conv_dt_proj_b, L1_conv_A_log, L1_conv_D_param, L1_conv_out_proj_w, L1_conv_proj_w, L1_conv_proj_b, L1_conv_skip_scale):
    import jax
    import jax.numpy as jnp
    def _L0_conv_ref(x, Wq, bq, Wk, bk, Wv, bv):
        import jax, jax.numpy as jnp
        import numpy as np
        import math
        B, C, H, W, S = (8, 512, 64, 64, 4)
        b, c, h, w = x.shape
        nb = h // S * (w // S)
        hw = h * w
        ss = S * S
        x_avg = x.reshape(b, c, h // S, S, w // S, S).mean(axis=(3, 5))
        x_avg = x_avg.reshape(b, c, nb).transpose(0, 2, 1)
        Q = x_avg @ Wq.T + bq
        K = x_avg @ Wk.T + bk
        A = jax.nn.softmax(jnp.einsum('bnc,bmc->bnm', Q, K) / jnp.sqrt(jnp.float32(c)), axis=-1)
        x_flat = x.reshape(b, c, hw).transpose(0, 2, 1)
        V = x_flat @ Wv.T + bv
        Vsum = V.reshape(b, hw // ss, ss, c).sum(axis=2)
        out_small = jnp.einsum('bnm,bmc->bnc', A, Vsum)
        out_flat = jnp.repeat(out_small, ss, axis=1)
        return out_flat.transpose(0, 2, 1).reshape(b, c, h, w)

    def _L1_conv_ref(x, norm_g, norm_b, in_proj_w, conv_w, conv_b, x_proj_w, dt_proj_w, dt_proj_b, A_log, D_param, out_proj_w, proj_w, proj_b, skip_scale):
        import jax, jax.numpy as jnp
        from jax import lax
        import numpy as np
        INPUT_DIM = 512
        OUTPUT_DIM = 512
        D_STATE = 16
        D_CONV = 4
        EXPAND = 2
        D_MODEL = INPUT_DIM // 4
        D_INNER = EXPAND * D_MODEL
        DT_RANK = (D_MODEL + 15) // 16
        EPS = 1e-05

        def layer_norm(x, g, b):
            mu = jnp.mean(x, axis=-1, keepdims=True)
            var = jnp.mean((x - mu) ** 2, axis=-1, keepdims=True)
            return (x - mu) * lax.rsqrt(var + EPS) * g + b

        def mamba(x, in_proj_w, conv_w, conv_b, x_proj_w, dt_proj_w, dt_proj_b, A_log, D_param, out_proj_w):
            Beff, L, _ = x.shape
            xz = jnp.einsum('bld,ed->ble', x, in_proj_w)
            xi, z = jnp.split(xz, 2, axis=-1)
            xc = lax.conv_general_dilated(xi.transpose(0, 2, 1), conv_w[:, None, :], (1,), [(D_CONV - 1, 0)], feature_group_count=D_INNER)
            xc = jax.nn.silu(xc + conv_b[None, :, None]).transpose(0, 2, 1)
            dbc = jnp.einsum('bld,ed->ble', xc, x_proj_w)
            dt = dbc[..., :DT_RANK]
            Bs = dbc[..., DT_RANK:DT_RANK + D_STATE]
            Cs = dbc[..., DT_RANK + D_STATE:]
            dt = jax.nn.softplus(jnp.einsum('blr,er->ble', dt, dt_proj_w) + dt_proj_b)
            A = -jnp.exp(A_log)

            def step(h, inp):
                dt_t, B_t, C_t, x_t = inp
                dA = jnp.exp(dt_t[:, :, None] * A)
                h = dA * h + (dt_t * x_t)[:, :, None] * B_t[:, None, :]
                y = jnp.einsum('bds,bs->bd', h, C_t)
                return (h, y)
            h0 = jnp.zeros((Beff, D_INNER, D_STATE), x.dtype)
            _, ys = lax.scan(step, h0, (dt.transpose(1, 0, 2), Bs.transpose(1, 0, 2), Cs.transpose(1, 0, 2), xc.transpose(1, 0, 2)))
            y = ys.transpose(1, 0, 2) + xc * D_param
            y = y * jax.nn.silu(z)
            return jnp.einsum('bld,od->blo', y, out_proj_w)
        B, C, H, W = x.shape
        L = H * W
        xf = x.reshape(B, C, L).transpose(0, 2, 1)
        xn = layer_norm(xf, norm_g, norm_b)
        chunks = xn.reshape(B, L, 4, D_MODEL).transpose(2, 0, 1, 3).reshape(4 * B, L, D_MODEL)
        ym = mamba(chunks, in_proj_w, conv_w, conv_b, x_proj_w, dt_proj_w, dt_proj_b, A_log, D_param, out_proj_w)
        ym = ym + skip_scale * chunks
        y = ym.reshape(4, B, L, D_MODEL).transpose(1, 2, 0, 3).reshape(B, L, C)
        y = layer_norm(y, norm_g, norm_b)
        y = jnp.einsum('blc,oc->blo', y, proj_w) + proj_b
        return y.transpose(0, 2, 1).reshape(B, OUTPUT_DIM, H, W)

    def _gn(v, G=32, eps=1e-5):
        B_, C_, H_, W_ = v.shape
        g = v.reshape(B_, G, C_ // G, H_, W_)
        m = jnp.mean(g, axis=(2, 3, 4), keepdims=True)
        s = jnp.var(g, axis=(2, 3, 4), keepdims=True)
        return ((g - m) / jnp.sqrt(s + eps)).reshape(v.shape)

    def _ln_c(v, eps=1e-6):
        m = jnp.mean(v, axis=1, keepdims=True)
        s = jnp.var(v, axis=1, keepdims=True)
        return (v - m) / jnp.sqrt(s + eps)

    def _ln_t(v, eps=1e-5):
        m = jnp.mean(v, axis=-1, keepdims=True)
        s = jnp.var(v, axis=-1, keepdims=True)
        return (v - m) / jnp.sqrt(s + eps)

    def _to_tokens(v):
        B_, C_, H_, W_ = v.shape
        return v.reshape(B_, C_, H_ * W_).transpose(0, 2, 1)
    def _from_tokens(t, like):
        B_, C_, H_, W_ = like.shape
        return t.transpose(0, 2, 1).reshape(B_, C_, H_, W_)

    x = x + _L0_conv_ref(_gn(x), L0_conv_Wq, L0_conv_bq, L0_conv_Wk, L0_conv_bk, L0_conv_Wv, L0_conv_bv)
    x = x + _L1_conv_ref(_gn(x), L1_conv_norm_g, L1_conv_norm_b, L1_conv_in_proj_w, L1_conv_conv_w, L1_conv_conv_b, L1_conv_x_proj_w, L1_conv_dt_proj_w, L1_conv_dt_proj_b, L1_conv_A_log, L1_conv_D_param, L1_conv_out_proj_w, L1_conv_proj_w, L1_conv_proj_b, L1_conv_skip_scale)
    return x


_drawn_inputs = setup_inputs


def setup_inputs(seed=0):
    import zlib

    import numpy as np

    out = dict(_drawn_inputs(seed))
    spreads = {'L1_conv_norm_g': (1.0, 0.2),
     'L1_conv_norm_b': (0.0, 0.1),
     'L1_conv_conv_b': (0.0, 0.8),
     'L1_conv_dt_proj_b': (-2.0, 0.6),
     'L1_conv_D_param': (1.0, 0.6),
     'L1_conv_proj_b': (0.0, 0.1)}
    factors = {'L0_conv_Wq': 8.0,
     'L0_conv_bq': 8.0,
     'L0_conv_Wk': 8.0,
     'L0_conv_bk': 8.0,
     'L1_conv_in_proj_w': 8.0,
     'L1_conv_conv_w': 8.0,
     'L1_conv_x_proj_w': 8.0,
     'L1_conv_dt_proj_w': 8.0,
     'L1_conv_A_log': 8.0,
     'L1_conv_out_proj_w': 8.0}
    for name, (base, spread) in spreads.items():
        noise = np.random.default_rng([zlib.crc32(name.encode()), seed]).standard_normal(out[name].shape)
        drawn = base * np.exp(spread * noise) if base else spread * noise
        out[name] = jnp.asarray(drawn.astype(out[name].dtype))
    for name, factor in factors.items():
        out[name] = (out[name] * factor).astype(out[name].dtype)
    return out
```

```python
from contextlib import ExitStack

import concourse.bass as bass
from concourse import mybir

F32 = mybir.dt.float32
BF16 = mybir.dt.bfloat16
ALU = mybir.AluOpType
ACT = mybir.ActivationFunctionType
AX_X = mybir.AxisListType.X
LN_EXP_SET = "natural_log_exp_and_others"

BATCH = 8
CH = 512
HW = 64
L = HW * HW
P = 128
NCH = CH // P
D_INNER = 256
NH = D_INNER // P
NS = 16
TAPS = 4
DT_RANK = 8
T = 512
NT = L // T
HALO = TAPS - 1
POOL = 4
SS = POOL * POOL
NB = L // SS
GROUP = 16
EPS = 1e-5
SMALL = 1.0 / 64
ATT_SCALE = float(CH) ** -0.5
STEPS = NCH * NS
ITEMS = NCH


def block_ssm_kernel(nc, x, wqkv, bq, bk, bv, norm_g, norm_b, w_in, conv_w, conv_b, w_x, w_dt, dt_b,
                     a_log, d_param, w_out, w_proj, proj_b, skip, eye, group_mean, row_select, out):
    with ExitStack() as ctx:
        def sb(name, shape, dt=F32):
            return ctx.enter_context(nc.sbuf_tensor(name, shape, dt))

        def pb(name, shape):
            return ctx.enter_context(nc.psum_tensor(name, shape, F32))

        def sem(name):
            return ctx.enter_context(nc.semaphore(name))

        X = sb("X", [P, NCH, L])
        XN = sb("XN", [P, NCH, 516])
        YB = sb("YB", [P, NCH, T])
        LV = sb("LV", [P, NCH, T])
        LS = sb("LS", [P, NCH, T])
        RS = sb("RS", [P, T])
        RING = sb("RING", [P, 7, NH, T])
        U, H, G = RING[:, 0:2], RING[:, 2:4], RING[:, 4:7]
        CS = sb("CS", [P, 2, T])
        ITEM = sb("ITEM", [P, 4, 2, NH, T])
        DT, DTX, XC, ZS = (ITEM[:, n] for n in range(4))
        SK = sb("SK", [P, T])
        YZ = sb("YZ", [P, NH, T])
        BC = sb("BC", [96, 2, T], BF16)
        RD = sb("RD", [64, T])
        R = RD
        DTR = RD[0:DT_RANK, :]
        EX = sb("EX", [P, NH, T])
        HS = sb("HS", [P, NCH, NH, NS])
        O = sb("O", [P, NCH, NB])
        WC = sb("WC", [P, TAPS, D_INNER])
        WZ = sb("WZ", [P, D_INNER])
        WX = sb("WX", [P, NH, 2 * NS + DT_RANK])
        WDT = sb("WDT", [DT_RANK, D_INNER])
        WO = sb("WO", [P, NH, P])
        WP = sb("WP", [P, NCH, CH])
        SEL = sb("SEL", [96, 2 * NS, P], BF16)
        EYE = sb("EYE", [P, P])
        MEAN = sb("MEAN", [P, P])
        GM = sb("GM", [P, P])
        AN = sb("AN", [P, NH, NS])
        COL = sb("COL", [P, 64])
        SM = sb("SM", [P, 96])
        ST = sb("ST", [P, NCH, NT, 6])
        SO = sb("SO", [P, NCH, 6])

        BQ, BK, BV = COL[:, 0:4], COL[:, 4:8], COL[:, 8:12]
        NG, NBI, PB = COL[:, 12:16], COL[:, 16:20], COL[:, 20:24]
        CB, DB, DP = COL[:, 24:26], COL[:, 26:28], COL[:, 28:30]
        SKIP, EPSC, BV16, PBF = COL[:, 30:31], COL[:, 31:32], COL[:, 32:36], COL[:, 36:40]
        NSMALL, ONESMALL, ZERO, LOGSMALL = (COL[:, n:n + 1] for n in range(40, 44))
        EM = YZ

        ring_flat = RING.rearrange("p a h t -> p (a h t)")
        S4 = ring_flat[:, 0:4096].rearrange("p (k h w) -> p k h w", k=NCH, h=HW)
        XA = ring_flat[:, 4096:5120].rearrange("p (k n) -> p k n", k=NCH)
        XS = ring_flat[:, 5120:6144].rearrange("p (k n) -> p k n", k=NCH)
        XSN = ring_flat[:, 0:1024].rearrange("p (k n) -> p k n", k=NCH)
        OC = ring_flat[:, 1024:2048].rearrange("p (k n) -> p k n", k=NCH)
        XSC = ring_flat[:, 2048:3072].rearrange("p (k n) -> p k n", k=NCH)
        OXP = ring_flat[:, 3072:4096].rearrange("p (k n) -> p k n", k=NCH)
        item_flat = ITEM.rearrange("p a b h t -> p (a b h t)")
        WQKV = item_flat[:, 0:3 * NCH * CH].rearrange("p (w k n) -> p w k n", w=3, k=NCH)
        lv_flat = LV.rearrange("p k t -> p (k t)")
        ls_flat = LS.rearrange("p k t -> p (k t)")
        Q = lv_flat[:, 0:1024].rearrange("p (k n) -> p k n", k=NCH)
        K = lv_flat[:, 1024:2048].rearrange("p (k n) -> p k n", k=NCH)
        VS = ls_flat[:, 0:1024].rearrange("p (m n) -> p m n", m=2)
        AT = ls_flat[:, 1024:1536].rearrange("p (m n) -> p m n", m=2)
        ATT = ls_flat[:, 1536:2048].rearrange("p (m n) -> p m n", m=2)
        MV = SM[:, 0:8].rearrange("p (k n) -> p k n", k=NCH)
        OV = SM[:, 8:16].rearrange("p (k n) -> p k n", k=NCH)
        DEV, GVAR, GLN, GRS, GSH, GRS16, GSH16 = (SM[:, 16 + 4 * n:20 + 4 * n] for n in range(7))
        MX, NMX, RSUM, RINV = (SM[:, 48 + 2 * n:50 + 2 * n] for n in range(4))
        COV, M1, V1 = (SM[:, 56 + 4 * n:60 + 4 * n] for n in range(3))
        A2, C2 = SM[:, 68:72], SM[:, 72:76]
        GSQ, GMS = SM[:, 76:80], SM[:, 80:84]

        DA = pb("DA", [P, NH, T])
        BP = pb("BP", [P, T])
        CP = pb("CP", [P, T])
        YP = pb("YP", [P, NH, T])
        FP = pb("FP", [P, 2, T])
        da_att = DA.rearrange("p h (a n) -> p (h a) n", n=NB)
        yp_att = YP.rearrange("p h (a n) -> p (h a) n", n=NB)

        w_loaded, x_loaded, wqkv_loaded, stored = (sem(n) for n in ("w_loaded", "x_loaded", "wqkv_loaded", "stored"))
        sel_cast, wc_ready, wp_folded, logsmall_ready, an_exp, an_ready, pbf_ps, pbf_ready, mean_ready = (
            sem(n) for n in ("sel_cast", "wc_ready", "wp_folded", "logsmall_ready", "an_exp", "an_ready", "pbf_ps", "pbf_ready", "mean_ready"))
        b_ready, u_ready, c_ready, c_copied, dA_ready, scanned, g_ready, state_kept, g_summed = (
            sem(n) for n in ("b_ready", "u_ready", "c_ready", "c_copied", "dA_ready", "scanned", "g_ready",
                             "state_kept", "g_summed"))
        (xi_ready, xi_copied, z_ready, xc_ready, zs_ready, skip_ready, dbc_ready, hi_ready, dtr_ready, rest_ready,
         mid_ready, lo_ready, dtp_ready, abs_ready, relu_ready, e_ready, l_ready, dt_ready, dtx_ready,
         yd_ready, yz_ready, out_ready, yb_ready, small_ready, excess_ready, square_ready, cubic_ready, poly_ready,
         large_ready) = (
            sem(n) for n in ("xi_ready", "xi_copied", "z_ready", "xc_ready", "zs_ready", "skip_ready", "dbc_ready",
                             "hi_ready", "dtr_ready", "rest_ready", "mid_ready", "lo_ready", "dtp_ready", "abs_ready",
                             "relu_ready", "e_ready", "l_ready", "dt_ready", "dtx_ready", "yd_ready", "yz_ready",
                             "out_ready", "yb_ready", "small_ready", "excess_ready", "square_ready", "cubic_ready",
                             "poly_ready", "large_ready"))
        (x1_ready, v_ready, mu1_ready, cen1_ready, sq1_ready, var1_ready, log1_ready, rstd1_ready, scaled1, halo_kept,
         xn_ready) = (
            sem(n) for n in ("x1_ready", "v_ready", "mu1_ready", "cen1_ready", "sq1_ready", "var1_ready",
                             "log1_ready", "rstd1_ready", "scaled1", "halo_kept", "xn_ready"))
        (mu2_ready, cen2_ready, sq2_ready, var2_ready, log2_ready, rstd2_ready, yn_ready, proj_ready, final_ready) = (
            sem(n) for n in ("mu2_ready", "cen2_ready", "sq2_ready", "var2_ready", "log2_ready", "rstd2_ready",
                             "yn_ready", "proj_ready", "final_ready"))
        (x_stats, x_aggr, s4_ready, pooled, gmean_ready, dev_ready, gvar_ready, glog_ready, grstd_ready, gshift_ready,
         pooled_norm, q_ps, k_ps, v_ps, q_ready, k_ready, v_ready_att, score_ps, max_ready, negmax_ready, prob_exp,
         rsum_inv, prob_ready, probT_ps, probT_ready, o_ps, o_ready, o_stats, o_aggr, o_centred, xs_centred, cov_ready,
         moments_ready, state_zeroed, chain) = (
            sem(n) for n in ("x_stats", "x_aggr", "s4_ready", "pooled", "gmean_ready", "dev_ready", "gvar_ready",
                             "glog_ready", "grstd_ready", "gshift_ready", "pooled_norm", "q_ps", "k_ps", "v_ps",
                             "q_ready", "k_ready", "v_ready_att", "score_ps", "max_ready", "negmax_ready", "prob_exp",
                             "rsum_inv", "prob_ready", "probT_ps", "probT_ready", "o_ps", "o_ready", "o_stats",
                             "o_aggr", "o_centred", "xs_centred", "cov_ready", "moments_ready", "state_zeroed", "chain"))

        block = ctx.enter_context(nc.Block())
        W_LOADS = 21
        CHAIN = 12


        def g_slot(n):
            return 1 if n % STEPS == STEPS - 1 else n % STEPS % 3

        def tokens(t, d):
            return bass.ds((t + d) * T, T)

        @block.sync
        def _(sp):
            def load_slice(b, t):
                sp.dma_start(X[:, :, bass.ds(t * T, T)],
                             x[b].rearrange("(k p) l -> p k l", p=P)[:, :, bass.ds(t * T, T)]).then_inc(x_loaded, 16)

            def load_qkv():
                for w in range(3):
                    sp.dma_start(WQKV[:, w], wqkv[w].rearrange("(k p) n -> p k n", p=P)).then_inc(wqkv_loaded, 16)

            def store_slice(b, t, tile):
                sp.wait_ge(final_ready, tile * NCH + NCH)
                sp.dma_start(out[b].rearrange("(k p) l -> p k l", p=P)[:, :, bass.ds(t * T, T)],
                             X[:, :, bass.ds(t * T, T)]).then_inc(stored, 16)

            for t in range(NT):
                load_slice(0, t)
            for dst, src in (
                    (COL[:, 0:4], bq), (COL[:, 4:8], bk), (COL[:, 8:12], bv), (COL[:, 12:16], norm_g),
                    (COL[:, 16:20], norm_b), (COL[:, 20:24], proj_b), (COL[:, 24:26], conv_b),
                    (COL[:, 26:28], dt_b), (COL[:, 28:30], d_param), (COL[:, 30:31], skip.broadcast_to([P, 1])),
                    (WZ[:, :], w_in[:, D_INNER:]), (WX[:, :, :], w_x.rearrange("(h p) n -> p h n", p=P)),
                    (WDT[:, :], w_dt), (WO[:, :, :], w_out.rearrange("(h p) n -> p h n", p=P)),
                    (WP[:, :, :], w_proj.rearrange("(k p) n -> p k n", p=P)), (EYE[:, :], eye),
                    (GM[:, :], group_mean), (AN[:, :, :], a_log.rearrange("(h p) s -> p h s", p=P)),
                    (YB[:, 0, 0:D_INNER], w_in[:, 0:D_INNER])):
                sp.dma_start(dst, src).then_inc(w_loaded, 16)
            sp.dma_start(YB[:, 1:3, :].rearrange("p a b -> p (a b)"),
                         conv_w.rearrange("(o k) e -> o (k e)", o=1).broadcast_to([P, TAPS * D_INNER])).then_inc(w_loaded, 16)
            sp.dma_start(ring_flat[0:96, 0:4096], row_select).then_inc(w_loaded, 16)
            load_qkv()

            with sp.Fori(0, BATCH - 1) as b:
                with sp.Fori(0, NT - 1) as t:
                    store_slice(b, t, b * NT + t)
                    sp.wait_ge(stored, b * (NT * 16) + t * 16 + 16)
                    load_slice(b + 1, t)
                sp.wait_ge(yz_ready, b * (NT * ITEMS) + NT * ITEMS)
                load_qkv()
                store_slice(b, NT - 1, b * NT + NT - 1)
                sp.wait_ge(stored, b * (NT * 16) + NT * 16)
                load_slice(b + 1, NT - 1)
            with sp.Fori(0, NT) as t:
                store_slice(BATCH - 1, t, t + (BATCH - 1) * NT)
            sp.wait_ge(stored, BATCH * NT * 16)

        @block.tensor
        def _(pe):
            def mm(*a, **k):
                return pe.matmul(*a, **k)

            def broadcast(tile, n, first=False):
                i, s = n // NS, n % NS
                if s == 0:
                    pe.wait_ge(lo_ready, tile * ITEMS + i + 1)
                if not first:
                    pe.wait_ge(u_ready, tile * STEPS + n)
                mm(BP[:, :], SEL[:, s, :], BC[:, i % 2, :], start=True, stop=True).then_inc(b_ready, 1)
                if not first:
                    pe.wait_ge(c_copied, tile * STEPS + n)
                mm(CP[:, :], SEL[:, NS + s, :], BC[:, i % 2, :], start=True, stop=True).then_inc(c_ready, 1)

            def state_sum(tile, n, first=False):
                i, s = n // NS, n % NS
                pe.wait_ge(g_ready, tile * STEPS + n + 1)
                if s == 0 and not first:
                    pe.wait_ge(yd_ready, tile * (2 * ITEMS) + 2 * i)
                for h in range(NH):
                    last = mm(YP[:, h, :], EYE[:, :], G[:, g_slot(n), h, :], start=(s == 0), stop=(s == NS - 1))
                last.then_inc(g_summed, 1)

            def xi_half(tile, i, h):
                if h == 0:
                    pe.wait_ge(xn_ready, tile + (i // ITEMS + 1))
                for k in range(TAPS):
                    last = mm(FP[:, h, :], WC[:, k, h * P:(h + 1) * P], XN[:, i % ITEMS, k:k + T],
                              start=(k == 0), stop=(k == TAPS - 1))
                last.then_inc(xi_ready, 1)

            def z_both(tile, i):
                pe.wait_ge(xi_copied, tile * (2 * ITEMS) + 2 * i + 2)
                for h in range(NH):
                    last = mm(FP[:, h, :], WZ[:, h * P:(h + 1) * P], XN[:, i % ITEMS, HALO:HALO + T],
                              start=True, stop=True)
                last.then_inc(z_ready, 1)

            def dbc(tile, i):
                pe.wait_ge(xc_ready, tile * ITEMS + i + 1)
                pe.wait_ge(zs_ready, tile * ITEMS + i + 1)
                for h in range(NH):
                    last = mm(FP[0:2 * NS + DT_RANK, 0, :], WX[:, h, :], XC[:, i % 2, h, :],
                              start=(h == 0), stop=(h == NH - 1))
                last.then_inc(dbc_ready, 1)

            def out_proj(tile, i):
                pe.wait_ge(yz_ready, tile * ITEMS + i + 1)
                for h in range(NH):
                    last = mm(FP[:, 1, :], WO[:, h, :], YZ[:, h, :], start=(h == 0), stop=(h == NH - 1))
                last.then_inc(out_ready, 1)

            def dt_proj(tile, i):
                pe.wait_ge(dtr_ready, tile * ITEMS + i + 1)
                pe.wait_ge(rest_ready, tile * ITEMS + i + 1)
                for h in range(NH):
                    last = mm(FP[:, h, :], WDT[:, h * P:(h + 1) * P], DTR[:, :], start=True, stop=True)
                last.then_inc(dtp_ready, 1)

            def channel_mean(bank, src, ready, ks):
                for k in ks:
                    last = mm(FP[:, bank, :], MEAN[:, :], src[:, k, :], start=(k == 0), stop=(k == NCH - 1))
                if k == NCH - 1:
                    last.then_inc(ready, 1)

            def proj(o, ks):
                for k in ks:
                    last = mm(FP[:, o % 2, :], WP[:, k, o * P:(o + 1) * P], LS[:, k, :],
                              start=(k == 0), stop=(k == NCH - 1))
                if k == NCH - 1:
                    last.then_inc(proj_ready, 1)

            def front_left(tile, i):
                pe.wait_ge(relu_ready, tile * (2 * ITEMS) + 2 * i + 2)
                pe.wait_ge(abs_ready, tile * (2 * ITEMS) + 2 * i + 2)

            def window(tile, w, first=False, front=True, ln1=True, ln2=True):
                j = w % ITEMS
                for s in range(NS):
                    n = w * NS + s
                    if front or s < NS - 1:
                        broadcast(tile, n + 1)
                    if s == 1 and front:
                        front_left(tile, w)
                        if j == 1 and ln2:
                            pe.wait_ge(log2_ready, tile + (w // ITEMS))
                        if j == 3 and ln1:
                            pe.wait_ge(log1_ready, tile + (w // ITEMS + 2))
                        xi_half(tile, w + 1, 0)
                    if s == 2 and front:
                        xi_half(tile, w + 1, 1)
                    if s == 4 and front:
                        z_both(tile, w + 1)
                    if s == 6:
                        if front:
                            dbc(tile, w + 1)
                        else:
                            front_left(tile, w)
                        if not first:
                            out_proj(tile, w - 1)
                    if s == 8 and front:
                        if not first:
                            pe.wait_ge(yb_ready, tile * ITEMS + w)
                        dt_proj(tile, w + 1)
                    if j == 0 and ln2:
                        if s == 10:
                            front_left(tile, w + 1)
                            pe.wait_ge(yb_ready, tile * ITEMS + w)
                            channel_mean(0, YB, mu2_ready, (0, 1))
                        if s == 11:
                            channel_mean(0, YB, mu2_ready, (2, 3))
                        if s == 14:
                            pe.wait_ge(sq2_ready, tile + w // ITEMS)
                            channel_mean(1, LS, var2_ready, range(NCH))
                    if j == 1 and ln2:
                        if s == 10:
                            front_left(tile, w + 1)
                            pe.wait_ge(yn_ready, tile + w // ITEMS)
                            proj(0, (0, 1))
                        if s == 11:
                            proj(0, (2, 3))
                        if s == 12:
                            proj(1, (0, 1))
                        if s == 13:
                            proj(1, (2, 3))
                        if s == 14:
                            pe.wait_ge(final_ready, (tile + (w // ITEMS - 1)) * NCH + 1)
                            proj(2, range(NCH))
                        if s == 15:
                            pe.wait_ge(final_ready, (tile + (w // ITEMS - 1)) * NCH + 2)
                            proj(3, range(NCH))
                    if j == 2 and ln1:
                        if s == 10:
                            front_left(tile, w + 1)
                            pe.wait_ge(v_ready, tile + (w // ITEMS + 2))
                            channel_mean(0, LV, mu1_ready, (0, 1))
                        if s == 11:
                            channel_mean(0, LV, mu1_ready, (2, 3))
                        if s == 14:
                            pe.wait_ge(sq1_ready, tile + (w // ITEMS + 2))
                            channel_mean(1, LS, var1_ready, range(NCH))
                    if s > 1 or not first:
                        state_sum(tile, n - 2, first=first and s == 2)

            def attention(b):
                pe.wait_ge(x_aggr, b + 1)
                mm(FP[:, 0, 0:NCH], GM[:, :], GMS[:, :], start=True, stop=True).then_inc(gmean_ready, 1)
                pe.wait_ge(dev_ready, b * 2 + 1)
                mm(FP[:, 1, 0:NCH], GM[:, :], GVAR[:, :], start=True, stop=True).then_inc(gvar_ready, 1)
                pe.wait_ge(wqkv_loaded, b * 48 + 48)
                pe.wait_ge(pooled_norm, b + 1)
                for w, dst, done in ((0, da_att, q_ps), (1, yp_att, k_ps)):
                    for o in range(NCH):
                        for k in range(NCH):
                            last = mm(dst[:, o, :], WQKV[:, w, k, o * P:(o + 1) * P], XA[:, k, :],
                                      start=(k == 0), stop=(k == NCH - 1), skip_group_check=True)
                    last.then_inc(done, 1)
                for m in range(2):
                    for k in range(NCH):
                        last = mm(FP[:, m, :], XSN[:, k, m * P:(m + 1) * P], WQKV[:, 2, k, :],
                                  start=(k == 0), stop=(k == NCH - 1))
                last.then_inc(v_ps, 1)
                pe.wait_ge(q_ready, b + 1)
                pe.wait_ge(k_ready, b + 1)
                for m, dst in enumerate((BP, CP)):
                    for k in range(NCH):
                        last = mm(dst[:, 0:NB], Q[:, k, m * P:(m + 1) * P], K[:, k, :],
                                  start=(k == 0), stop=(k == NCH - 1))
                last.then_inc(score_ps, 1)
                pe.wait_ge(prob_ready, b + 1)
                for m in range(2):
                    for n in range(2):
                        last = pe.transpose(DA[:, m, n * P:(n + 1) * P], AT[:, n, m * P:(m + 1) * P], EYE[:, :])
                last.then_inc(probT_ps, 1)
                pe.wait_ge(v_ready_att, b + 1)
                pe.wait_ge(probT_ready, b + 1)
                for o in range(NCH):
                    for m in range(2):
                        last = mm(yp_att[:, o, :], VS[:, m, o * P:(o + 1) * P], ATT[:, m, :],
                                  start=(m == 0), stop=(m == 1), skip_group_check=True)
                last.then_inc(o_ps, 1)
                pe.wait_ge(moments_ready, b + 1)
                mm(FP[:, 0, 0:NCH], GM[:, :], M1[:, :], start=True, stop=True).then_inc(gmean_ready, 1)
                pe.wait_ge(dev_ready, b * 2 + 2)
                mm(FP[:, 1, 0:NCH], GM[:, :], GVAR[:, :], start=True, stop=True).then_inc(gvar_ready, 1)

            def first_front(tile):
                pe.wait_ge(v_ready, tile + 1)
                channel_mean(0, LV, mu1_ready, range(NCH))
                pe.wait_ge(sq1_ready, tile + 1)
                channel_mean(1, LS, var1_ready, range(NCH))
                pe.wait_ge(log1_ready, tile + 1)
                xi_half(tile, 0, 0)
                xi_half(tile, 0, 1)
                z_both(tile, 0)
                dbc(tile, 0)
                dt_proj(tile, 0)
                broadcast(tile, 0, first=True)

            def last_end(tile):
                state_sum(tile, STEPS - 2)
                state_sum(tile, STEPS - 1)
                pe.wait_ge(yb_ready, tile * ITEMS + (ITEMS - 1))
                out_proj(tile, ITEMS - 1)
                pe.wait_ge(yb_ready, tile * ITEMS + ITEMS)
                channel_mean(0, YB, mu2_ready, range(NCH))
                pe.wait_ge(sq2_ready, tile + 1)
                channel_mean(1, LS, var2_ready, range(NCH))
                pe.wait_ge(yn_ready, tile + 1)
                proj(0, range(NCH))
                proj(1, range(NCH))
                pe.wait_ge(final_ready, tile * NCH + 1)
                proj(2, range(NCH))
                pe.wait_ge(final_ready, tile * NCH + 2)
                proj(3, range(NCH))

            pe.wait_ge(w_loaded, 16 * W_LOADS)
            for o in range(NCH):
                for k in range(NCH):
                    last = mm(FP[:, 0, o:o + 1], WP[:, k, o * P:(o + 1) * P], NBI[:, k:k + 1],
                              start=(k == 0), stop=(k == NCH - 1), skip_group_check=True)
            last.then_inc(pbf_ps, 1)
            pe.wait_ge(pbf_ready, 1)
            pe.wait_ge(wp_folded, NCH)
            pe.wait_ge(wc_ready, TAPS)
            pe.wait_ge(sel_cast, 1)
            pe.wait_ge(mean_ready, 1)
            with pe.Fori(0, BATCH) as b:
                attention(b)
                first_front(b * NT)
                window(b * NT, 0, first=True, ln2=False)
                window(b * NT, 1, ln2=False)
                with pe.Fori(0, NT - 1) as t:
                    for w in range(2, 2 + ITEMS):
                        window(b * NT + t, w)
                window(b * NT + (NT - 1), 2, ln1=False)
                window(b * NT + (NT - 1), 3, ln1=False, front=False)
                last_end(b * NT + (NT - 1))

        @block.scalar
        def _(act):
            def step(tile, n, first=False):
                i, s = n // NS, n % NS
                if s == 0:
                    act.wait_ge(dt_ready, tile * ITEMS + i + 1)
                act.wait_ge(c_ready, tile * STEPS + n + 1)
                if not (first and s < 2):
                    act.wait_ge(g_ready, tile * STEPS + (n - 1))
                act.activation(CS[:, n % 2, :], CP[:, :], ACT.Copy).then_inc(c_copied, 1)
                for h in range(NH):
                    if not (first and s == 0):
                        act.wait_ge(scanned, tile * (2 * STEPS) + (2 * n - 1 + h))
                    act.activation(DA[:, h, :], DT[:, i % 2, h, :], ACT.Exp, scale=AN[:, h, s:s + 1]).then_inc(dA_ready, 1)

            def xi_copy(tile, i, h):
                act.wait_ge(xi_ready, tile * (2 * ITEMS) + 2 * i + h + 1)
                act.activation(XC[:, i % 2, h, :], FP[:, h, :], ACT.Identity, bias=CB[:, h:h + 1]).then_inc(xi_copied, 1)

            def silus(tile, i):
                act.wait_ge(xi_copied, tile * (2 * ITEMS) + 2 * i + 2)
                act.activation(XC[:, i % 2], XC[:, i % 2], ACT.Silu).then_inc(xc_ready, 1)
                act.wait_ge(z_ready, tile * ITEMS + i + 1)
                act.activation(ZS[:, i % 2], FP[:, :, :], ACT.Silu).then_inc(zs_ready, 1)
                act.preload_act_table_set(LN_EXP_SET)

            def dbc_copy(tile, i):
                act.wait_ge(dbc_ready, tile * ITEMS + i + 1)
                act.activation(BC[0:32, i % 2, :], FP[0:32, 0, :], ACT.Copy).then_inc(hi_ready, 1)
                act.activation(DTR[:, :], FP[32:32 + DT_RANK, 0, :], ACT.Copy).then_inc(dtr_ready, 1)

            def mid(tile, i):
                act.wait_ge(rest_ready, tile * ITEMS + i + 1)
                act.activation(BC[32:64, i % 2, :], R[32:64, :], ACT.Copy).then_inc(mid_ready, 1)

            def dt_abs(tile, i):
                act.wait_ge(dtp_ready, tile * ITEMS + i + 1)
                for h in range(NH):
                    act.activation(DTX[:, i % 2, h, :], FP[:, h, :], ACT.Abs, bias=DB[:, h:h + 1]).then_inc(abs_ready, 1)

            def dt_exp(tile, i):
                act.wait_ge(abs_ready, tile * (2 * ITEMS) + 2 * i + 2)
                act.activation(DTX[:, i % 2], DTX[:, i % 2], ACT.Exp, scale=-1.0).then_inc(e_ready, 1)

            def dt_excess(tile, i):
                act.wait_ge(e_ready, tile * ITEMS + i + 1)
                act.activation(EX[:, :, :], DTX[:, i % 2], ACT.Relu, bias=NSMALL).then_inc(excess_ready, 1)

            def dt_log(tile, i):
                act.wait_ge(excess_ready, tile * ITEMS + i + 1)
                act.activation(EX[:, :, :], EX[:, :, :], ACT.Ln, bias=ONESMALL).then_inc(l_ready, 1)

            def skip_term(tile, i):
                dst = SK[:, :] if i % ITEMS == 0 else YB[:, i % ITEMS, :]
                act.activation(dst, XN[:, i % ITEMS, HALO:HALO + T], ACT.Copy,
                               scale=SKIP[:, 0:1]).then_inc(skip_ready, 1)

            def square(cen, sq, v):
                act.wait_ge(cen, v)
                act.activation(LS[:, :, :], LV[:, :, :], ACT.Square).then_inc(sq, 1)

            def rstd(var, log, done, v):
                act.wait_ge(var, v)
                act.activation(RS[:, :], FP[:, 1, :], ACT.Ln, bias=EPSC[:, 0:1]).then_inc(log, 1)
                act.wait_ge(log, v)
                act.activation(RS[:, :], RS[:, :], ACT.Exp, scale=-0.5).then_inc(done, 1)

            def window(tile, w, first=False, front=True, ln1=True, ln2=True):
                j = w % ITEMS
                for s in range(NS):
                    step(tile, w * NS + s, first=first)
                    if front:
                        if s == 2:
                            if not first:
                                act.wait_ge(yd_ready, tile * (2 * ITEMS) + 2 * w)
                            xi_copy(tile, w + 1, 0)
                        if s == 3:
                            xi_copy(tile, w + 1, 1)
                        if s == 5:
                            if not first:
                                act.wait_ge(yz_ready, tile * ITEMS + w)
                            silus(tile, w + 1)
                        if s == 7:
                            dbc_copy(tile, w + 1)
                        if s == 8:
                            mid(tile, w + 1)
                        if s == 9:
                            dt_abs(tile, w + 1)
                        if s == 10:
                            dt_exp(tile, w + 1)
                            dt_excess(tile, w + 1)
                        if s == 11:
                            dt_log(tile, w + 1)
                        if s == 13:
                            if j == 0 and ln2:
                                act.wait_ge(cen2_ready, tile + w // ITEMS)
                            skip_term(tile, w + 1)
                    if j == 0 and ln2:
                        if s == 13:
                            square(cen2_ready, sq2_ready, tile + w // ITEMS)
                        if s == 15:
                            rstd(var2_ready, log2_ready, rstd2_ready, tile + w // ITEMS)
                    if j == 2 and ln1:
                        if s == 13:
                            square(cen1_ready, sq1_ready, tile + (w // ITEMS + 2))
                        if s == 15:
                            rstd(var1_ready, log1_ready, rstd1_ready, tile + (w // ITEMS + 2))

            def attention(b):
                def group_rstd(n):
                    act.wait_ge(gvar_ready, b * 2 + n)
                    act.activation(GLN[:, :], FP[:, 1, 0:NCH], ACT.Ln, bias=EPSC[:, 0:1]).then_inc(glog_ready, 1)
                    act.wait_ge(glog_ready, b * 2 + n)
                    act.activation(GRS[:, :], GLN[:, :], ACT.Exp, scale=-0.5).then_inc(grstd_ready, 1)

                act.preload_act_table_set(LN_EXP_SET)
                group_rstd(1)
                for dst, src, bias, ps, done in ((Q, da_att, BQ, q_ps, q_ready), (K, yp_att, BK, k_ps, k_ready)):
                    act.wait_ge(ps, b + 1)
                    for o in range(NCH):
                        last = act.activation(dst[:, o, :], src[:, o, :], ACT.Identity, bias=bias[:, o:o + 1])
                    last.then_inc(done, 1)
                act.wait_ge(v_ps, b + 1)
                act.activation(VS[:, :, :], FP[:, :, :], ACT.Copy).then_inc(v_ready_att, 1)
                act.wait_ge(negmax_ready, b + 1)
                for m, src in enumerate((BP, CP)):
                    last = act.activation(AT[:, m, :], src[:, 0:NB], ACT.Exp, scale=ATT_SCALE,
                                          bias=NMX[:, m:m + 1], accum_out=RSUM[:, m:m + 1])
                last.then_inc(prob_exp, 1)
                act.wait_ge(probT_ps, b + 1)
                act.activation(ATT[:, :, :], DA[:, :, 0:NB], ACT.Copy).then_inc(probT_ready, 1)
                act.wait_ge(o_ps, b + 1)
                for o in range(NCH):
                    last = act.activation(O[:, o, :], yp_att[:, o, :], ACT.Identity, bias=BV16[:, o:o + 1])
                last.then_inc(o_ready, 1)
                group_rstd(2)

            def first_front(tile):
                square(cen1_ready, sq1_ready, tile + 1)
                rstd(var1_ready, log1_ready, rstd1_ready, tile + 1)
                xi_copy(tile, 0, 0)
                xi_copy(tile, 0, 1)
                silus(tile, 0)
                dbc_copy(tile, 0)
                mid(tile, 0)
                dt_abs(tile, 0)
                dt_exp(tile, 0)
                dt_excess(tile, 0)
                dt_log(tile, 0)
                skip_term(tile, 0)

            def last_end(tile):
                square(cen2_ready, sq2_ready, tile + 1)
                rstd(var2_ready, log2_ready, rstd2_ready, tile + 1)

            act.wait_ge(w_loaded, 16 * W_LOADS)
            act.preload_act_table_set(LN_EXP_SET)
            act.activation(AN[:, :, :], AN[:, :, :], ACT.Exp).then_inc(an_exp, 1)
            act.wait_ge(mean_ready, 6)
            act.activation(LOGSMALL, ZERO, ACT.Ln, bias=ONESMALL).then_inc(logsmall_ready, 1)
            act.wait_ge(an_ready, 1)
            with act.Fori(0, BATCH) as b:
                attention(b)
                first_front(b * NT)
                window(b * NT, 0, first=True, ln2=False)
                window(b * NT, 1, ln2=False)
                with act.Fori(0, NT - 1) as t:
                    for w in range(2, 2 + ITEMS):
                        window(b * NT + t, w)
                window(b * NT + (NT - 1), 2, ln1=False)
                window(b * NT + (NT - 1), 3, ln1=False, front=False)
                last_end(b * NT + (NT - 1))

        @block.vector
        def _(dve):
            def make_u(tile, n, first=False):
                i, s = n // NS, n % NS
                if s == 0:
                    dve.wait_ge(dtx_ready, tile * ITEMS + i + 1)
                dve.wait_ge(b_ready, tile * STEPS + n + 1)
                if not (first and s < 2):
                    dve.wait_ge(scanned, tile * (2 * STEPS) + (2 * n - 2))
                dve.tensor_tensor(U[:, n % 2], DTX[:, i % 2], BP[:, :].unsqueeze(1).broadcast_to([P, NH, T]),
                                  ALU.mult).then_inc(u_ready, 1)

            def scan(tile, n, first=False):
                i, s = n // NS, n % NS
                dve.wait_ge(u_ready, tile * STEPS + n + 1)
                if not (first and s < 2):
                    dve.wait_ge(state_kept, tile * STEPS + (n - 1))
                for h in range(NH):
                    dve.wait_ge(dA_ready, tile * (2 * STEPS) + (2 * n + h + 1))
                    dve.tensor_tensor_scan(H[:, n % 2, h, :], DA[:, h, :], U[:, n % 2, h, :],
                                           HS[:, i % ITEMS, h, s:s + 1], ALU.mult, ALU.add).then_inc(scanned, 1)

            def y_and_d(tile, i):
                dve.wait_ge(g_summed, tile * STEPS + NS * (i + 1))
                for h in range(NH):
                    dve.scalar_tensor_tensor(out=YZ[:, h, :], in0=XC[:, i % 2, h, :], scalar=DP[:, h:h + 1],
                                             in1=YP[:, h, :], op0=ALU.mult, op1=ALU.add).then_inc(yd_ready, 1)

            def bc_rest(tile, i):
                dve.wait_ge(hi_ready, tile * ITEMS + i + 1)
                dve.wait_ge(dtr_ready, tile * ITEMS + i + 1)
                dve.tensor_tensor(R[32:64, :], FP[0:32, 0, :], BC[0:32, i % 2, :], ALU.subtract).then_inc(rest_ready, 1)

            def bc_lo(tile, i):
                dve.wait_ge(mid_ready, tile * ITEMS + i + 1)
                dve.tensor_tensor(BC[64:96, i % 2, :], R[32:64, :], BC[32:64, i % 2, :], ALU.subtract).then_inc(lo_ready, 1)

            def add_skip(tile, i):
                dve.wait_ge(out_ready, tile * ITEMS + i + 1)
                dve.wait_ge(skip_ready, tile * ITEMS + i + 1)
                skip_part = SK[:, :] if i % ITEMS == 0 else YB[:, i % ITEMS, :]
                dve.tensor_tensor(YB[:, i % ITEMS, :], skip_part, FP[:, 1, :], ALU.add).then_inc(yb_ready, 1)

            def dt_relu(tile, i):
                dve.wait_ge(dtp_ready, tile * ITEMS + i + 1)
                for h in range(NH):
                    dve.wait_ge(abs_ready, tile * (2 * ITEMS) + (2 * i + h + 1))
                    dve.tensor_scalar(DT[:, i % 2, h, :], FP[:, h, :], DB[:, h:h + 1], 0.0,
                                      ALU.add, ALU.max).then_inc(relu_ready, 1)

            def dt_small(tile, i):
                dve.wait_ge(e_ready, tile * ITEMS + i + 1)
                dve.tensor_scalar(EM[:, :, :], DTX[:, i % 2], SMALL, None, ALU.min).then_inc(small_ready, 1)

            def dt_poly(tile, i):
                v = tile * ITEMS + i + 1
                dve.wait_ge(small_ready, v)
                dve.wait_ge(excess_ready, v)
                dve.scalar_tensor_tensor(out=DTX[:, i % 2], in0=EM[:, :, :], scalar=1.0 / 3, in1=EM[:, :, :],
                                         op0=ALU.mult, op1=ALU.mult).then_inc(square_ready, 1)
                dve.wait_ge(square_ready, v)
                dve.scalar_tensor_tensor(out=DTX[:, i % 2], in0=EM[:, :, :], scalar=-0.5, in1=DTX[:, i % 2],
                                         op0=ALU.mult, op1=ALU.add).then_inc(cubic_ready, 1)

            def dt_large(tile, i):
                v = tile * ITEMS + i + 1
                dve.wait_ge(cubic_ready, v)
                dve.scalar_tensor_tensor(out=DTX[:, i % 2], in0=DTX[:, i % 2], scalar=1.0, in1=EM[:, :, :],
                                         op0=ALU.add, op1=ALU.mult).then_inc(poly_ready, 1)
                dve.wait_ge(l_ready, v)
                dve.wait_ge(relu_ready, tile * (2 * ITEMS) + 2 * i + 2)
                dve.scalar_tensor_tensor(out=DT[:, i % 2], in0=EX[:, :, :], scalar=LOGSMALL, in1=DT[:, i % 2],
                                         op0=ALU.subtract, op1=ALU.add).then_inc(large_ready, 1)

            def centre(src, mu, done, v):
                dve.wait_ge(mu, v)
                dve.tensor_tensor(LV[:, :, :], src[:, :, :], FP[:, 0, :].unsqueeze(1).broadcast_to([P, NCH, T]),
                                  ALU.subtract).then_inc(done, 1)

            def add_attention(t, d):
                blocks = T // SS
                xt = X[:, :, tokens(t, d)].rearrange("p k (m q) -> p k m q", q=SS)
                ot = O[:, :, bass.ds((t + d) * blocks, blocks)].unsqueeze(3).broadcast_to([P, NCH, blocks, SS])
                dve.tensor_tensor(xt, xt, ot, ALU.add).then_inc(x1_ready, 1)

            def group_norm(t, d, v):
                dve.wait_ge(x1_ready, v)
                for k in range(NCH):
                    last = dve.tensor_scalar(LV[:, k, :], X[:, k, tokens(t, d)], A2[:, k:k + 1], C2[:, k:k + 1],
                                             ALU.mult, ALU.add)
                last.then_inc(v_ready, 1)

            def apply_norm(v, first=False):
                if first:
                    dve.memset(XN[:, :, 0:HALO], 0.0).then_inc(halo_kept, 1)
                else:
                    dve.tensor_copy(XN[:, :, 0:HALO], XN[:, :, T:T + HALO]).then_inc(halo_kept, 1)
                dve.wait_ge(rstd1_ready, v)
                dve.tensor_tensor(LV[:, :, :], LV[:, :, :], RS[:, :].unsqueeze(1).broadcast_to([P, NCH, T]),
                                  ALU.mult).then_inc(scaled1, 1)
                dve.wait_ge(scaled1, v)
                dve.wait_ge(halo_kept, v)
                for k in range(NCH):
                    last = dve.tensor_scalar(XN[:, k, HALO:HALO + T], LV[:, k, :], NG[:, k:k + 1], NBI[:, k:k + 1],
                                             ALU.mult, ALU.add)
                last.then_inc(xn_ready, 1)

            def finish(t, d, o, v):
                dve.wait_ge(proj_ready, v * NCH + (o + 1))
                xt = X[:, o, tokens(t, d)]
                dve.scalar_tensor_tensor(out=xt, in0=FP[:, o % 2, :], scalar=PBF[:, o:o + 1], in1=xt,
                                         op0=ALU.add, op1=ALU.add).then_inc(final_ready, 1)

            def window(tile, w, t, first=False, front=True, ln1=True, ln2=True):
                j = w % ITEMS
                for s in range(NS):
                    n = w * NS + s
                    if front or s < NS - 1:
                        make_u(tile, n + 1, first=first and n + 1 < 2)
                    scan(tile, n, first=first)
                    if j == 3 and ln1 and s == 0:
                        dve.wait_ge(skip_ready, tile * ITEMS + w + 1)
                        apply_norm(tile + (w // ITEMS + 2))
                    if s == 2 and not first:
                        y_and_d(tile, w - 1)
                    if s == 7:
                        if front:
                            bc_rest(tile, w + 1)
                        if not first:
                            add_skip(tile, w - 1)
                    if front:
                        if s == 8:
                            bc_lo(tile, w + 1)
                        if s == 9:
                            dt_relu(tile, w + 1)
                        if s == 10:
                            dt_small(tile, w + 1)
                        if s == 11:
                            dt_poly(tile, w + 1)
                        if s == 12:
                            dt_large(tile, w + 1)
                    if j == 0 and ln2 and s == 12:
                        centre(YB, mu2_ready, cen2_ready, tile + w // ITEMS)
                    if j == 1 and ln2:
                        if s == 12:
                            finish(t, w // ITEMS - 1, 0, tile + (w // ITEMS - 1))
                        if s == 14:
                            finish(t, w // ITEMS - 1, 1, tile + (w // ITEMS - 1))
                        if s == 15:
                            finish(t, w // ITEMS - 1, 2, tile + (w // ITEMS - 1))
                            finish(t, w // ITEMS - 1, 3, tile + (w // ITEMS - 1))
                    if j == 2 and ln1:
                        if s == 3:
                            add_attention(t, w // ITEMS + 1)
                        if s == 4:
                            group_norm(t, w // ITEMS + 1, tile + (w // ITEMS + 2))
                        if s == 12:
                            centre(LV, mu1_ready, cen1_ready, tile + (w // ITEMS + 2))

            def attention(b):
                def group_moments(n, mean, var, scale, shift):
                    dve.wait_ge(gmean_ready, b * 2 + n)
                    dve.tensor_tensor(DEV[:, :], mean, FP[:, 0, 0:NCH], ALU.subtract).then_inc(chain, 1)
                    link()
                    dve.tensor_tensor(GSQ[:, :], DEV[:, :], DEV[:, :], ALU.mult).then_inc(chain, 1)
                    link()
                    dve.tensor_tensor(GVAR[:, :], GSQ[:, :], var, ALU.add).then_inc(dev_ready, 1)
                    dve.wait_ge(grstd_ready, b * 2 + n)
                    dve.tensor_copy(scale, GRS[:, :]).then_inc(chain, 1)
                    link()
                    dve.scalar_tensor_tensor(out=shift, in0=FP[:, 0, 0:NCH], scalar=-1.0, in1=GRS[:, :],
                                             op0=ALU.mult, op1=ALU.mult).then_inc(gshift_ready, 1)
                    dve.wait_ge(gshift_ready, b * 2 + n)

                links = [0]

                def link():
                    links[0] += 1
                    dve.wait_ge(chain, b * CHAIN + links[0])

                dve.memset(HS[:, :, :, :], 0.0).then_inc(state_zeroed, 1)
                dve.wait_ge(x_loaded, b * (NT * 16) + 16 * NT)
                for t in range(NT):
                    for k in range(NCH):
                        last = dve.bn_stats(ST[:, k, t, :], X[:, k, t * T:(t + 1) * T])
                last.then_inc(x_stats, 1)
                for k in range(NCH):
                    if k == 1:
                        dve.wait_ge(x_stats, b + 1)
                    last = dve.tensor_reduce(S4[:, k], X[:, k, :].rearrange("p (h w q) -> p h w q", h=HW, q=POOL),
                                             AX_X, ALU.add)
                last.then_inc(s4_ready, 1)
                for k in range(NCH):
                    last = dve.bn_aggr(MV[:, k, :], ST[:, k].rearrange("p t n -> p (t n)"))
                last.then_inc(chain, 1)
                link()
                dve.tensor_copy(GMS[:, :], MV[:, :, 0]).then_inc(x_aggr, 1)
                dve.wait_ge(s4_ready, b + 1)
                for k in range(NCH):
                    dve.tensor_reduce(XS[:, k, :], S4[:, k].rearrange("p h (w q) -> p (h w) q", q=POOL), AX_X, ALU.add)
                    last = dve.tensor_reduce(XA[:, k, :].rearrange("p (h w) -> p h w", h=HW // POOL),
                                             S4[:, k].rearrange("p (h q) w -> p h w q", q=POOL), AX_X, ALU.add)
                last.then_inc(pooled, 1)
                dve.wait_ge(x_aggr, b + 1)
                group_moments(1, GMS[:, :], MV[:, :, 1], GRS16[:, :], GSH[:, :])
                dve.tensor_scalar(GRS16[:, :], GRS16[:, :], 1.0 / SS, None, ALU.mult).then_inc(chain, 1)
                dve.tensor_scalar(GSH16[:, :], GSH[:, :], float(SS), None, ALU.mult).then_inc(chain, 1)
                links[0] += 1
                link()
                dve.wait_ge(pooled, b + 1)
                for k in range(NCH):
                    dve.tensor_scalar(XSN[:, k, :], XS[:, k, :], GRS[:, k:k + 1], GSH16[:, k:k + 1], ALU.mult, ALU.add)
                    last = dve.tensor_scalar(XA[:, k, :], XA[:, k, :], GRS16[:, k:k + 1], GSH[:, k:k + 1],
                                             ALU.mult, ALU.add)
                last.then_inc(pooled_norm, 1)
                dve.wait_ge(score_ps, b + 1)
                for m, src in enumerate((BP, CP)):
                    last = dve.tensor_reduce(MX[:, m:m + 1], src[:, 0:NB], AX_X, ALU.max)
                last.then_inc(max_ready, 1)
                dve.wait_ge(max_ready, b + 1)
                dve.tensor_scalar(NMX[:, :], MX[:, :], -ATT_SCALE, None, ALU.mult).then_inc(negmax_ready, 1)
                dve.wait_ge(prob_exp, b + 1)
                dve.reciprocal(RINV[:, :], RSUM[:, :]).then_inc(rsum_inv, 1)
                dve.wait_ge(rsum_inv, b + 1)
                for m in range(2):
                    last = dve.tensor_scalar(AT[:, m, :], AT[:, m, :], RINV[:, m:m + 1], None, ALU.mult)
                last.then_inc(prob_ready, 1)
                dve.wait_ge(o_ready, b + 1)
                for k in range(NCH):
                    last = dve.bn_stats(SO[:, k, :], O[:, k, :])
                last.then_inc(o_stats, 1)
                dve.wait_ge(o_stats, b + 1)
                for k in range(NCH):
                    last = dve.tensor_scalar(XSC[:, k, :], XS[:, k, :], 1.0 / SS, MV[:, k, 0:1], ALU.mult, ALU.subtract)
                last.then_inc(xs_centred, 1)
                for k in range(NCH):
                    last = dve.bn_aggr(OV[:, k, :], SO[:, k, :])
                last.then_inc(o_aggr, 1)
                dve.wait_ge(o_aggr, b + 1)
                for k in range(NCH):
                    last = dve.tensor_scalar(OC[:, k, :], O[:, k, :], OV[:, k, 0:1], None, ALU.subtract)
                last.then_inc(o_centred, 1)
                dve.wait_ge(o_centred, b + 1)
                dve.wait_ge(xs_centred, b + 1)
                dve.tensor_tensor(OXP[:, :, :], OC[:, :, :], XSC[:, :, :], ALU.mult).then_inc(chain, 1)
                link()
                dve.tensor_reduce(COV[:, :], OXP[:, :, :], AX_X, ALU.add).then_inc(cov_ready, 1)
                dve.tensor_tensor(M1[:, :], MV[:, :, 0], OV[:, :, 0], ALU.add).then_inc(chain, 1)
                dve.wait_ge(cov_ready, b + 1)
                dve.scalar_tensor_tensor(out=V1[:, :], in0=COV[:, :], scalar=2.0 / NB, in1=MV[:, :, 1],
                                         op0=ALU.mult, op1=ALU.add).then_inc(chain, 1)
                links[0] += 1
                link()
                dve.tensor_tensor(V1[:, :], V1[:, :], OV[:, :, 1], ALU.add).then_inc(moments_ready, 1)
                dve.wait_ge(moments_ready, b + 1)
                group_moments(2, M1[:, :], V1[:, :], A2[:, :], C2[:, :])
                assert links[0] == CHAIN

            def first_front(tile, image):
                add_attention(0, 0)
                group_norm(0, 0, tile + 1)
                centre(LV, mu1_ready, cen1_ready, tile + 1)
                apply_norm(tile + 1, first=True)
                bc_rest(tile, 0)
                bc_lo(tile, 0)
                dt_relu(tile, 0)
                dt_small(tile, 0)
                dt_poly(tile, 0)
                dt_large(tile, 0)
                make_u(tile, 0, first=True)
                dve.wait_ge(state_zeroed, image + 1)

            def last_end(tile):
                y_and_d(tile, ITEMS - 1)
                add_skip(tile, ITEMS - 1)
                centre(YB, mu2_ready, cen2_ready, tile + 1)
                for o in range(NCH):
                    finish(0, NT - 1, o, tile)

            dve.wait_ge(w_loaded, 16 * W_LOADS)
            dve.memset(MEAN[:, :], 1.0 / CH).then_inc(mean_ready, 1)
            dve.memset(EPSC, EPS).then_inc(mean_ready, 1)
            dve.memset(NSMALL, -SMALL).then_inc(mean_ready, 1)
            dve.memset(ONESMALL, 1.0 + SMALL).then_inc(mean_ready, 1)
            dve.memset(ZERO, 0.0).then_inc(mean_ready, 1)
            dve.tensor_scalar(BV16, BV, float(SS), None, ALU.mult).then_inc(mean_ready, 1)
            dve.tensor_copy(SEL[:, :, :].rearrange("p a b -> p (a b)"), ring_flat[0:96, 0:4096]).then_inc(sel_cast, 1)
            taps = YB[:, 1:3, :].rearrange("p a b -> p (a b)").rearrange("p (k e) -> p k e", k=TAPS)
            for k in range(TAPS):
                dve.tensor_tensor(WC[:, k, :], YB[:, 0, 0:D_INNER], taps[:, k, :], ALU.mult).then_inc(wc_ready, 1)
            dve.wait_ge(logsmall_ready, 1)
            dve.wait_ge(an_exp, 1)
            dve.tensor_scalar(AN[:, :, :], AN[:, :, :], -1.0, None, ALU.mult).then_inc(an_ready, 1)
            dve.wait_ge(pbf_ps, 1)
            dve.tensor_tensor(PBF, PB, FP[:, 0, 0:NCH], ALU.add).then_inc(pbf_ready, 1)
            for k in range(NCH):
                dve.tensor_scalar(WP[:, k, :], WP[:, k, :], NG[:, k:k + 1], None, ALU.mult).then_inc(wp_folded, 1)
            dve.wait_ge(sel_cast, 1)
            dve.wait_ge(wc_ready, TAPS)
            dve.wait_ge(pbf_ready, 1)
            dve.wait_ge(wp_folded, NCH)
            with dve.Fori(0, BATCH) as b:
                attention(b)
                first_front(b * NT, b)
                window(b * NT, 0, 0, first=True, ln2=False)
                window(b * NT, 1, 0, ln2=False)
                with dve.Fori(0, NT - 1) as t:
                    for w in range(2, 2 + ITEMS):
                        window(b * NT + t, w, t)
                window(b * NT + (NT - 1), 2, NT - 1, ln1=False)
                window(b * NT + (NT - 1), 3, NT - 1, ln1=False, front=False)
                last_end(b * NT + (NT - 1))
                dve.wait_ge(g_summed, (b + 1) * (NT * STEPS))
                dve.wait_ge(state_kept, (b + 1) * (NT * STEPS))
                dve.wait_ge(scanned, (b + 1) * (2 * NT * STEPS))
                dve.wait_ge(final_ready, (b + 1) * (NT * NCH))

        @block.gpsimd
        def _(pool):
            def step(tile, n, first=False):
                i, s = n // NS, n % NS
                pool.wait_ge(c_copied, tile * STEPS + n + 1)
                if not (first and s < 3):
                    used = 2 if n % STEPS in (1, STEPS - 1) else 3
                    pool.wait_ge(g_summed, tile * STEPS + (n - used + 1))
                pool.wait_ge(scanned, tile * (2 * STEPS) + 2 * (n + 1))
                pool.tensor_tensor(G[:, g_slot(n)], H[:, n % 2], CS[:, n % 2, :].unsqueeze(1).broadcast_to([P, NH, T]),
                                   ALU.mult).then_inc(g_ready, 1)
                pool.tensor_copy(HS[:, i % ITEMS, :, s:s + 1], H[:, n % 2, :, T - 1:T]).then_inc(state_kept, 1)

            def gate(tile, i):
                pool.wait_ge(yd_ready, tile * (2 * ITEMS) + 2 * (i + 1))
                pool.tensor_tensor(YZ[:, :, :], YZ[:, :, :], ZS[:, i % 2], ALU.mult).then_inc(yz_ready, 1)

            def dt_sum(tile, i):
                pool.wait_ge(poly_ready, tile * ITEMS + i + 1)
                pool.wait_ge(large_ready, tile * ITEMS + i + 1)
                pool.tensor_tensor(DT[:, i % 2], DT[:, i % 2], DTX[:, i % 2], ALU.add).then_inc(dt_ready, 1)

            def dt_x(tile, i):
                pool.wait_ge(dt_ready, tile * ITEMS + i + 1)
                pool.tensor_tensor(DTX[:, i % 2], DT[:, i % 2], XC[:, i % 2], ALU.mult).then_inc(dtx_ready, 1)

            def normalise(v):
                pool.wait_ge(rstd2_ready, v)
                pool.tensor_tensor(LS[:, :, :], LV[:, :, :], RS[:, :].unsqueeze(1).broadcast_to([P, NCH, T]),
                                   ALU.mult).then_inc(yn_ready, 1)

            def window(tile, w, first=False, front=True, ln2=True):
                j = w % ITEMS
                for s in range(NS):
                    step(tile, w * NS + s, first=first)
                    if s == 3 and not first:
                        gate(tile, w - 1)
                    if s == 4 and j == 1 and ln2:
                        normalise(tile + w // ITEMS)
                    if front:
                        if s == 12:
                            dt_sum(tile, w + 1)
                        if s == 13:
                            dt_x(tile, w + 1)

            with pool.Fori(0, BATCH) as b:
                dt_sum(b * NT, 0)
                dt_x(b * NT, 0)
                window(b * NT, 0, first=True)
                window(b * NT, 1, ln2=False)
                with pool.Fori(0, NT - 1) as t:
                    for w in range(2, 2 + ITEMS):
                        window(b * NT + t, w)
                window(b * NT + (NT - 1), 2)
                window(b * NT + (NT - 1), 3, front=False)
                gate(b * NT + (NT - 1), ITEMS - 1)
                normalise(b * NT + NT)


INPUTS = {
    "x": (BATCH, CH, L), "wqkv": (3, CH, CH), "bq": (P, NCH), "bk": (P, NCH), "bv": (P, NCH), "norm_g": (P, NCH),
    "norm_b": (P, NCH), "w_in": (P, 2 * D_INNER), "conv_w": (TAPS, D_INNER), "conv_b": (P, NH),
    "w_x": (D_INNER, 2 * NS + DT_RANK), "w_dt": (DT_RANK, D_INNER), "dt_b": (P, NH), "a_log": (D_INNER, NS),
    "d_param": (P, NH), "w_out": (D_INNER, P), "w_proj": (CH, CH), "proj_b": (P, NCH), "skip": (1, 1),
    "eye": (P, P), "group_mean": (P, P), "row_select": (96, 2 * NS * P),
}


def kernel(**inputs):
    import numpy as np
    import concourse.bacc as bacc
    from concourse.bass_utils import run_bass_kernel_spmd

    a = {k: np.asarray(v) for k, v in inputs.items()}

    def columns(v):
        return v.reshape(-1, P).T

    x_proj = a["L1_conv_x_proj_w"]
    rows = np.arange(96)[:, None] % (2 * NS) == np.arange(2 * NS)[None, :]
    laid_out = {
        "x": a["x"].reshape(BATCH, CH, L),
        "wqkv": np.stack([a["L0_conv_Wq"].T, a["L0_conv_Wk"].T, a["L0_conv_Wv"].T]),
        "bq": columns(a["L0_conv_bq"]), "bk": columns(a["L0_conv_bk"]), "bv": columns(a["L0_conv_bv"]),
        "norm_g": columns(a["L1_conv_norm_g"]), "norm_b": columns(a["L1_conv_norm_b"]),
        "w_in": a["L1_conv_in_proj_w"].T, "conv_w": a["L1_conv_conv_w"].T, "conv_b": columns(a["L1_conv_conv_b"]),
        "w_x": np.concatenate([x_proj[DT_RANK:], x_proj[:DT_RANK]]).T,
        "w_dt": a["L1_conv_dt_proj_w"].T, "dt_b": columns(a["L1_conv_dt_proj_b"]),
        "a_log": a["L1_conv_A_log"], "d_param": columns(a["L1_conv_D_param"]), "w_out": a["L1_conv_out_proj_w"].T,
        "w_proj": a["L1_conv_proj_w"].T, "proj_b": columns(a["L1_conv_proj_b"]),
        "skip": a["L1_conv_skip_scale"].reshape(1, 1),
        "eye": np.eye(P, dtype=np.float32),
        "group_mean": np.kron(np.eye(P // GROUP, dtype=np.float32), np.full((GROUP, GROUP), 1.0 / GROUP, np.float32)),
        "row_select": np.repeat(rows.astype(np.float32), P, axis=1),
    }
    nc = bacc.Bacc("TRN2", target_bir_lowering=False, num_devices=1)
    arrays, aps = {}, {}
    for name, shape in INPUTS.items():
        arrays[f"in_{name}"] = np.ascontiguousarray(laid_out[name])
        assert arrays[f"in_{name}"].shape == shape
        aps[name] = nc.dram_tensor(f"in_{name}", shape, F32, kind="ExternalInput").ap()
    out = nc.dram_tensor("out", (BATCH, CH, L), F32, kind="ExternalOutput").ap()
    block_ssm_kernel(nc, out=out, **aps)
    r = run_bass_kernel_spmd(nc, [arrays], core_ids=[0])
    return r.results[0]["out"].reshape(BATCH, CH, HW, HW)
```

```python
from contextlib import ExitStack

import concourse.bass as bass
from concourse import mybir

F32 = mybir.dt.float32
BF16 = mybir.dt.bfloat16
ALU = mybir.AluOpType
ACT = mybir.ActivationFunctionType
AX_X = mybir.AxisListType.X
LN_EXP_SET = "natural_log_exp_and_others"

BATCH = 8
CH = 512
HW = 64
L = HW * HW
P = 128
NCH = CH // P
D_INNER = 256
NH = D_INNER // P
NS = 16
TAPS = 4
DT_RANK = 8
T = 512
NT = L // T
HALO = TAPS - 1
POOL = 4
SS = POOL * POOL
NB = L // SS
GROUP = 16
EPS = 1e-5
SMALL = 1.0 / 64
ATT_SCALE = float(CH) ** -0.5
STEPS = NCH * NS
ITEMS = NCH


def block_ssm_kernel(nc, x, wqkv, bq, bk, bv, norm_g, norm_b, w_in, conv_w, conv_b, w_x, w_dt, dt_b,
                     a_log, d_param, w_out, w_proj, proj_b, skip, eye, group_mean, row_select, out):
    with ExitStack() as ctx:
        def sb(name, shape, dt=F32):
            return ctx.enter_context(nc.sbuf_tensor(name, shape, dt))

        def pb(name, shape):
            return ctx.enter_context(nc.psum_tensor(name, shape, F32))

        def sem(name):
            return ctx.enter_context(nc.semaphore(name))

        X = sb("X", [P, NCH, L])
        XN = sb("XN", [P, NCH, 516])
        YB = sb("YB", [P, NCH, T])
        LV = sb("LV", [P, NCH, T])
        LS = sb("LS", [P, NCH, T])
        RS = sb("RS", [P, T])
        RING = sb("RING", [P, 7, NH, T])
        U, H, G = RING[:, 0:2], RING[:, 2:4], RING[:, 4:7]
        CS = sb("CS", [P, 2, T])
        ITEM = sb("ITEM", [P, 4, 2, NH, T])
        DT, DTX, XC, ZS = (ITEM[:, n] for n in range(4))
        SK = sb("SK", [P, T])
        YZ = sb("YZ", [P, NH, T])
        BC = sb("BC", [96, 2, T], BF16)
        RD = sb("RD", [64, T])
        R = RD
        DTR = RD[0:DT_RANK, :]
        EX = sb("EX", [P, NH, T])
        HS = sb("HS", [P, NCH, NH, NS])
        O = sb("O", [P, NCH, NB])
        WC = sb("WC", [P, TAPS, D_INNER])
        WZ = sb("WZ", [P, D_INNER])
        WX = sb("WX", [P, NH, 2 * NS + DT_RANK])
        WDT = sb("WDT", [DT_RANK, D_INNER])
        WO = sb("WO", [P, NH, P])
        WP = sb("WP", [P, NCH, CH])
        SEL = sb("SEL", [96, 2 * NS], BF16)
        DA = sb("DA", [P, 2, NH, T])
        EYE = sb("EYE", [P, P])
        MEAN = sb("MEAN", [P, P])
        GM = sb("GM", [P, P])
        AN = sb("AN", [P, NH, NS])
        COL = sb("COL", [P, 64])
        SM = sb("SM", [P, 96])
        ST = sb("ST", [P, NCH, NT, 6])
        SO = sb("SO", [P, NCH, 6])

        BQ, BK, BV = COL[:, 0:4], COL[:, 4:8], COL[:, 8:12]
        NG, NBI, PB = COL[:, 12:16], COL[:, 16:20], COL[:, 20:24]
        CB, DB, DP = COL[:, 24:26], COL[:, 26:28], COL[:, 28:30]
        SKIP, EPSC, BV16, PBF = COL[:, 30:31], COL[:, 31:32], COL[:, 32:36], COL[:, 36:40]
        NSMALL, ONESMALL, ZERO, NLOGSMALL = (COL[:, n:n + 1] for n in range(40, 44))
        EM = YZ

        ring_flat = RING.rearrange("p a h t -> p (a h t)")
        S4 = ring_flat[:, 0:4096].rearrange("p (k h w) -> p k h w", k=NCH, h=HW)
        XA = ring_flat[:, 4096:5120].rearrange("p (k n) -> p k n", k=NCH)
        XS = ring_flat[:, 5120:6144].rearrange("p (k n) -> p k n", k=NCH)
        XSN = ring_flat[:, 0:1024].rearrange("p (k n) -> p k n", k=NCH)
        OC = ring_flat[:, 1024:2048].rearrange("p (k n) -> p k n", k=NCH)
        XSC = ring_flat[:, 2048:3072].rearrange("p (k n) -> p k n", k=NCH)
        OXP = ring_flat[:, 3072:4096].rearrange("p (k n) -> p k n", k=NCH)
        item_flat = ITEM.rearrange("p a b h t -> p (a b h t)")
        WQKV = item_flat[:, 0:3 * NCH * CH].rearrange("p (w k n) -> p w k n", w=3, k=NCH)
        lv_flat = LV.rearrange("p k t -> p (k t)")
        ls_flat = LS.rearrange("p k t -> p (k t)")
        Q = lv_flat[:, 0:1024].rearrange("p (k n) -> p k n", k=NCH)
        K = lv_flat[:, 1024:2048].rearrange("p (k n) -> p k n", k=NCH)
        VS = ls_flat[:, 0:1024].rearrange("p (m n) -> p m n", m=2)
        AT = ls_flat[:, 1024:1536].rearrange("p (m n) -> p m n", m=2)
        ATT = ls_flat[:, 1536:2048].rearrange("p (m n) -> p m n", m=2)
        MV = SM[:, 0:8].rearrange("p (k n) -> p k n", k=NCH)
        OV = SM[:, 8:16].rearrange("p (k n) -> p k n", k=NCH)
        DEV, GVAR, GLN, GRS, GSH, GRS16, GSH16 = (SM[:, 16 + 4 * n:20 + 4 * n] for n in range(7))
        MX, NMX, RSUM, RINV = (SM[:, 48 + 2 * n:50 + 2 * n] for n in range(4))
        COV, M1, V1 = (SM[:, 56 + 4 * n:60 + 4 * n] for n in range(3))
        A2, C2 = SM[:, 68:72], SM[:, 72:76]
        GSQ, GMS = SM[:, 76:80], SM[:, 80:84]

        BP = pb("BP", [P, 2, T])
        CP = pb("CP", [P, T])
        YP = pb("YP", [P, NH, T])
        FP = pb("FP", [P, 2, T])
        LP = pb("LP", [P, T])
        bp_att = BP.rearrange("p h (a n) -> p (h a) n", n=NB)
        yp_att = YP.rearrange("p h (a n) -> p (h a) n", n=NB)

        w_loaded, x_early, x_last, wqkv_loaded, stored = (
            sem(n) for n in ("w_loaded", "x_early", "x_last", "wqkv_loaded", "stored"))
        sel_cast, wc_ready, wp_folded, logsmall_ready, an_exp, an_ready, pbf_ps, pbf_ready, mean_ready = (
            sem(n) for n in ("sel_cast", "wc_ready", "wp_folded", "logsmall_ready", "an_exp", "an_ready", "pbf_ps", "pbf_ready", "mean_ready"))
        b_ready, u_ready, c_ready, c_copied, dA_ready, scanned, g_ready, state_kept, g_summed = (
            sem(n) for n in ("b_ready", "u_ready", "c_ready", "c_copied", "dA_ready", "scanned", "g_ready",
                             "state_kept", "g_summed"))
        (xi_ready, xi_copied, z_ready, xc_ready, zs_ready, skip_ready, dbc_ready, hi_ready, dtr_ready, rest_ready,
         mid_ready, lo_ready, dtp_ready, abs_ready, relu_ready, e_ready, l_ready, dt_ready, dtx_ready,
         yd_ready, yz_ready, out_ready, yb_ready, small_ready, excess_ready, square_ready, cubic_ready, poly_ready,
         large_ready, dt_begun) = (
            sem(n) for n in ("xi_ready", "xi_copied", "z_ready", "xc_ready", "zs_ready", "skip_ready", "dbc_ready",
                             "hi_ready", "dtr_ready", "rest_ready", "mid_ready", "lo_ready", "dtp_ready", "abs_ready",
                             "relu_ready", "e_ready", "l_ready", "dt_ready", "dtx_ready", "yd_ready", "yz_ready",
                             "out_ready", "yb_ready", "small_ready", "excess_ready", "square_ready", "cubic_ready",
                             "poly_ready", "large_ready", "dt_begun"))
        (x1_ready, v_ready, mu1_ready, cen1_ready, sq1_ready, var1_ready, log1_ready, rstd1_ready, scaled1, halo_kept,
         xn_ready) = (
            sem(n) for n in ("x1_ready", "v_ready", "mu1_ready", "cen1_ready", "sq1_ready", "var1_ready",
                             "log1_ready", "rstd1_ready", "scaled1", "halo_kept", "xn_ready"))
        (mu2_ready, cen2_ready, sq2_ready, var2_ready, log2_ready, rstd2_ready, yn_ready, proj_ready, final_ready) = (
            sem(n) for n in ("mu2_ready", "cen2_ready", "sq2_ready", "var2_ready", "log2_ready", "rstd2_ready",
                             "yn_ready", "proj_ready", "final_ready"))
        (x_stats, x_aggr, s4_early, s4_ready, pooled, gmean_ready, dev_ready, gvar_ready, glog_ready, grstd_ready, gshift_ready,
         pooled_norm, q_ps, k_ps, v_ps, q_ready, k_ready, v_ready_att, score_ps, max_ready, negmax_ready, prob_exp,
         rsum_inv, prob_ready, probT_ps, probT_ready, o_ps, o_ready, o_stats, o_aggr, o_centred, xs_centred, cov_ready,
         moments_ready, state_zeroed, chain) = (
            sem(n) for n in ("x_stats", "x_aggr", "s4_early", "s4_ready", "pooled", "gmean_ready", "dev_ready", "gvar_ready",
                             "glog_ready", "grstd_ready", "gshift_ready", "pooled_norm", "q_ps", "k_ps", "v_ps",
                             "q_ready", "k_ready", "v_ready_att", "score_ps", "max_ready", "negmax_ready", "prob_exp",
                             "rsum_inv", "prob_ready", "probT_ps", "probT_ready", "o_ps", "o_ready", "o_stats",
                             "o_aggr", "o_centred", "xs_centred", "cov_ready", "moments_ready", "state_zeroed", "chain"))

        block = ctx.enter_context(nc.Block())
        W_LOADS = 21
        CHAIN = 12


        def g_slot(n):
            return 1 if n % STEPS == STEPS - 1 else n % STEPS % 3

        def out_step(j):
            return 8 if j == 2 else 7

        def proj_bank(o):
            return LP[:, :] if o < 2 else FP[:, o - 2, :]

        def tokens(t, d):
            return bass.ds((t + d) * T, T)

        def attention_views(t, d):
            blocks = T // SS
            return (X[:, :, tokens(t, d)].rearrange("p k (m q) -> p k m q", q=SS),
                    O[:, :, bass.ds((t + d) * blocks, blocks)].unsqueeze(3).broadcast_to([P, NCH, blocks, SS]))

        @block.sync
        def _(sp):
            def load_slice(b, t, loaded=x_early):
                sp.dma_start(X[:, :, bass.ds(t * T, T)],
                             x[b].rearrange("(k p) l -> p k l", p=P)[:, :, bass.ds(t * T, T)]).then_inc(loaded, 16)

            def load_qkv():
                for w in range(3):
                    sp.dma_start(WQKV[:, w], wqkv[w].rearrange("(k p) n -> p k n", p=P)).then_inc(wqkv_loaded, 16)

            def store_slice(b, t, tile):
                sp.wait_ge(final_ready, tile * NCH + NCH)
                sp.dma_start(out[b].rearrange("(k p) l -> p k l", p=P)[:, :, bass.ds(t * T, T)],
                             X[:, :, bass.ds(t * T, T)]).then_inc(stored, 16)

            for t in range(NT - 1):
                load_slice(0, t)
            load_slice(0, NT - 1, x_last)
            for dst, src in (
                    (COL[:, 0:4], bq), (COL[:, 4:8], bk), (COL[:, 8:12], bv), (COL[:, 12:16], norm_g),
                    (COL[:, 16:20], norm_b), (COL[:, 20:24], proj_b), (COL[:, 24:26], conv_b),
                    (COL[:, 26:28], dt_b), (COL[:, 28:30], d_param), (COL[:, 30:31], skip.broadcast_to([P, 1])),
                    (WZ[:, :], w_in[:, D_INNER:]), (WX[:, :, :], w_x.rearrange("(h p) n -> p h n", p=P)),
                    (WDT[:, :], w_dt), (WO[:, :, :], w_out.rearrange("(h p) n -> p h n", p=P)),
                    (WP[:, :, :], w_proj.rearrange("(k p) n -> p k n", p=P)), (EYE[:, :], eye),
                    (GM[:, :], group_mean), (AN[:, :, :], a_log.rearrange("(h p) s -> p h s", p=P)),
                    (YB[:, 0, 0:D_INNER], w_in[:, 0:D_INNER])):
                sp.dma_start(dst, src).then_inc(w_loaded, 16)
            sp.dma_start(YB[:, 1:3, :].rearrange("p a b -> p (a b)"),
                         conv_w.rearrange("(o k) e -> o (k e)", o=1).broadcast_to([P, TAPS * D_INNER])).then_inc(w_loaded, 16)
            sp.dma_start(ring_flat[0:96, 0:2 * NS], row_select).then_inc(w_loaded, 16)
            load_qkv()

            with sp.Fori(0, BATCH - 1) as b:
                with sp.Fori(0, NT - 1) as t:
                    store_slice(b, t, b * NT + t)
                    sp.wait_ge(stored, b * (NT * 16) + t * 16 + 16)
                    load_slice(b + 1, t)
                sp.wait_ge(yz_ready, b * (NT * ITEMS) + NT * ITEMS)
                load_qkv()
                store_slice(b, NT - 1, b * NT + NT - 1)
                sp.wait_ge(stored, b * (NT * 16) + NT * 16)
                load_slice(b + 1, NT - 1, x_last)
            with sp.Fori(0, NT) as t:
                store_slice(BATCH - 1, t, t + (BATCH - 1) * NT)
            sp.wait_ge(stored, BATCH * NT * 16)

        @block.tensor
        def _(pe):
            def mm(*a, **k):
                return pe.matmul(*a, **k)

            def broadcast_b(tile, n, first=False):
                i, s = n // NS, n % NS
                if s == 0:
                    pe.wait_ge(lo_ready, tile * ITEMS + i + 1)
                if not first:
                    pe.wait_ge(u_ready, tile * STEPS + n - 1)
                mm(BP[:, n % 2, :], SEL[:, s:s + 1].broadcast_to([96, P]), BC[:, i % 2, :],
                   start=True, stop=True).then_inc(b_ready, 1)

            def broadcast_c(tile, n, first=False):
                i, s = n // NS, n % NS
                if not first:
                    pe.wait_ge(c_copied, tile * STEPS + n)
                mm(CP[:, :], SEL[:, NS + s:NS + s + 1].broadcast_to([96, P]), BC[:, i % 2, :],
                   start=True, stop=True).then_inc(c_ready, 1)

            def state_sum(tile, n, first=False):
                i, s = n // NS, n % NS
                pe.wait_ge(g_ready, tile * STEPS + n + 1)
                if s == 0 and not first:
                    pe.wait_ge(yd_ready, tile * (2 * ITEMS) + 2 * i)
                for h in range(NH):
                    last = mm(YP[:, h, :], EYE[:, :], G[:, g_slot(n), h, :], start=(s == 0), stop=(s == NS - 1))
                last.then_inc(g_summed, 1)

            def xi_half(tile, i, h, taps=range(TAPS)):
                if h == 0:
                    pe.wait_ge(xn_ready, tile + (i // ITEMS + 1))
                for k in taps:
                    last = mm(FP[:, h, :], WC[:, k, h * P:(h + 1) * P], XN[:, i % ITEMS, k:k + T],
                              start=(k == 0), stop=(k == TAPS - 1))
                if k == TAPS - 1:
                    last.then_inc(xi_ready, 1)

            def z_both(tile, i):
                pe.wait_ge(xi_copied, tile * (2 * ITEMS) + 2 * i + 2)
                for h in range(NH):
                    last = mm(FP[:, h, :], WZ[:, h * P:(h + 1) * P], XN[:, i % ITEMS, HALO:HALO + T],
                              start=True, stop=True)
                last.then_inc(z_ready, 1)

            def dbc(tile, i):
                pe.wait_ge(xc_ready, tile * ITEMS + i + 1)
                pe.wait_ge(zs_ready, tile * ITEMS + i + 1)
                for h in range(NH):
                    last = mm(FP[0:2 * NS + DT_RANK, 0, :], WX[:, h, :], XC[:, i % 2, h, :],
                              start=(h == 0), stop=(h == NH - 1))
                last.then_inc(dbc_ready, 1)

            def out_proj(tile, i):
                pe.wait_ge(yz_ready, tile * ITEMS + i + 1)
                for h in range(NH):
                    last = mm(LP[:, :], WO[:, h, :], YZ[:, h, :], start=(h == 0), stop=(h == NH - 1))
                last.then_inc(out_ready, 1)

            def dt_proj(tile, i):
                pe.wait_ge(dtr_ready, tile * ITEMS + i + 1)
                pe.wait_ge(rest_ready, tile * ITEMS + i + 1)
                for h in range(NH):
                    last = mm(FP[:, h, :], WDT[:, h * P:(h + 1) * P], DTR[:, :], start=True, stop=True)
                last.then_inc(dtp_ready, 1)

            def channel_mean(src, ready, ks):
                for k in ks:
                    last = mm(LP[:, :], MEAN[:, :], src[:, k, :], start=(k == 0), stop=(k == NCH - 1))
                if k == NCH - 1:
                    last.then_inc(ready, 1)

            def proj(o, ks):
                for k in ks:
                    last = mm(proj_bank(o), WP[:, k, o * P:(o + 1) * P], LS[:, k, :],
                              start=(k == 0), stop=(k == NCH - 1))
                if k == NCH - 1:
                    last.then_inc(proj_ready, 1)

            def front_left(tile, i):
                pe.wait_ge(relu_ready, tile * (2 * ITEMS) + 2 * i + 2)
                pe.wait_ge(abs_ready, tile * (2 * ITEMS) + 2 * i + 2)

            def window(tile, w, first=False, front=True, ln1=True, ln2=True):
                j = w % ITEMS
                for s in range(NS):
                    n = w * NS + s
                    if front or s < NS - 2:
                        broadcast_b(tile, n + 2)
                    broadcast_c(tile, n, first=first and s == 0)
                    if front:
                        if s == 0:
                            front_left(tile, w)
                            xi_half(tile, w + 1, 0, (0, 1))
                        if s == 1:
                            xi_half(tile, w + 1, 0, (2, 3))
                        if s == 2:
                            xi_half(tile, w + 1, 1, (0, 1))
                        if s == 3:
                            xi_half(tile, w + 1, 1, (2, 3))
                        if s == 4:
                            z_both(tile, w + 1)
                        if s == 6:
                            dbc(tile, w + 1)
                        if s == 8:
                            dt_proj(tile, w + 1)
                    if j == 0 and ln2:
                        if s == 10:
                            pe.wait_ge(yb_ready, tile * ITEMS + w)
                            channel_mean(YB, mu2_ready, (0, 1))
                        if s == 11:
                            channel_mean(YB, mu2_ready, (2, 3))
                        if s == 14:
                            pe.wait_ge(sq2_ready, tile + w // ITEMS)
                            channel_mean(LS, var2_ready, (0, 1))
                        if s == 15:
                            channel_mean(LS, var2_ready, (2, 3))
                    if j == 1 and ln2:
                        if s == 4:
                            pe.wait_ge(log2_ready, tile + w // ITEMS)
                            pe.wait_ge(yn_ready, tile + w // ITEMS)
                            proj(0, (0, 1))
                        if s == 5:
                            proj(0, (2, 3))
                        if s == 7:
                            pe.wait_ge(final_ready, (tile + (w // ITEMS - 1)) * NCH + 1)
                        if s == 9:
                            pe.wait_ge(yb_ready, tile * ITEMS + w)
                            proj(1, (0, 1))
                        if s == 10:
                            proj(1, (2, 3))
                        if s == 11:
                            front_left(tile, w + 1)
                            proj(2, (0, 1))
                        if s == 12:
                            proj(2, (2, 3))
                        if s == 13:
                            proj(3, (0, 1))
                        if s == 14:
                            proj(3, (2, 3))
                    if j == 2 and ln1:
                        if s == 5:
                            pe.wait_ge(v_ready, tile + w // ITEMS + 2)
                            channel_mean(LV, mu1_ready, (0, 1))
                        if s == 6:
                            channel_mean(LV, mu1_ready, (2, 3))
                        if s == 8:
                            pe.wait_ge(cen1_ready, tile + w // ITEMS + 2)
                        if s == 10:
                            pe.wait_ge(yb_ready, tile * ITEMS + w)
                            pe.wait_ge(sq1_ready, tile + w // ITEMS + 2)
                            channel_mean(LS, var1_ready, (0, 1))
                        if s == 11:
                            channel_mean(LS, var1_ready, (2, 3))
                    if j == 3 and ln1 and s == 7:
                        pe.wait_ge(log1_ready, tile + w // ITEMS + 2)
                    if s == out_step(j) and not first:
                        out_proj(tile, w - 1)
                    if s > 1 or not first:
                        state_sum(tile, n - 2, first=first and s == 2)

            def attention(b):
                pe.wait_ge(x_aggr, b + 1)
                mm(FP[:, 0, 0:NCH], GM[:, :], GMS[:, :], start=True, stop=True).then_inc(gmean_ready, 1)
                pe.wait_ge(dev_ready, b * 2 + 1)
                mm(FP[:, 1, 0:NCH], GM[:, :], GVAR[:, :], start=True, stop=True).then_inc(gvar_ready, 1)
                pe.wait_ge(wqkv_loaded, b * 48 + 48)
                pe.wait_ge(pooled_norm, b + 1)
                for w, dst, done in ((0, bp_att, q_ps), (1, yp_att, k_ps)):
                    for o in range(NCH):
                        for k in range(NCH):
                            last = mm(dst[:, o, :], WQKV[:, w, k, o * P:(o + 1) * P], XA[:, k, :],
                                      start=(k == 0), stop=(k == NCH - 1), skip_group_check=True)
                    last.then_inc(done, 1)
                def values(m):
                    for k in range(NCH):
                        last = mm(FP[:, m, :], XSN[:, k, m * P:(m + 1) * P], WQKV[:, 2, k, :],
                                  start=(k == 0), stop=(k == NCH - 1))
                    return last

                values(0)
                pe.wait_ge(q_ready, b + 1)
                pe.wait_ge(k_ready, b + 1)
                for m in range(2):
                    for k in range(NCH):
                        last = mm(CP[:, m * NB:(m + 1) * NB], Q[:, k, m * P:(m + 1) * P], K[:, k, :],
                                  start=(k == 0), stop=(k == NCH - 1))
                last.then_inc(score_ps, 1)
                values(1).then_inc(v_ps, 1)
                pe.wait_ge(prob_ready, b + 1)
                for m in range(2):
                    for n in range(2):
                        last = pe.transpose(BP[:, m, n * P:(n + 1) * P], AT[:, n, m * P:(m + 1) * P], EYE[:, :])
                last.then_inc(probT_ps, 1)
                pe.wait_ge(v_ready_att, b + 1)
                pe.wait_ge(probT_ready, b + 1)
                for o in range(NCH):
                    for m in range(2):
                        last = mm(yp_att[:, o, :], VS[:, m, o * P:(o + 1) * P], ATT[:, m, :],
                                  start=(m == 0), stop=(m == 1), skip_group_check=True)
                last.then_inc(o_ps, 1)
                pe.wait_ge(moments_ready, b + 1)
                mm(FP[:, 0, 0:NCH], GM[:, :], M1[:, :], start=True, stop=True).then_inc(gmean_ready, 1)
                pe.wait_ge(dev_ready, b * 2 + 2)
                mm(FP[:, 1, 0:NCH], GM[:, :], GVAR[:, :], start=True, stop=True).then_inc(gvar_ready, 1)

            def first_front(tile):
                pe.wait_ge(v_ready, tile + 1)
                channel_mean(LV, mu1_ready, range(NCH))
                pe.wait_ge(sq1_ready, tile + 1)
                channel_mean(LS, var1_ready, range(NCH))
                xi_half(tile, 0, 0)
                xi_half(tile, 0, 1)
                z_both(tile, 0)
                dbc(tile, 0)
                dt_proj(tile, 0)
                broadcast_b(tile, 0, first=True)
                broadcast_b(tile, 1, first=True)

            def last_end(tile):
                state_sum(tile, STEPS - 2)
                state_sum(tile, STEPS - 1)
                out_proj(tile, ITEMS - 1)
                pe.wait_ge(yb_ready, tile * ITEMS + ITEMS)
                channel_mean(YB, mu2_ready, range(NCH))
                pe.wait_ge(sq2_ready, tile + 1)
                channel_mean(LS, var2_ready, range(NCH))
                pe.wait_ge(log2_ready, tile + 1)
                pe.wait_ge(yn_ready, tile + 1)
                proj(0, range(NCH))
                pe.wait_ge(final_ready, tile * NCH + 1)
                proj(1, range(NCH))
                proj(2, range(NCH))
                proj(3, range(NCH))

            pe.wait_ge(w_loaded, 16 * W_LOADS)
            for o in range(NCH):
                for k in range(NCH):
                    last = mm(FP[:, 0, o:o + 1], WP[:, k, o * P:(o + 1) * P], NBI[:, k:k + 1],
                              start=(k == 0), stop=(k == NCH - 1), skip_group_check=True)
            last.then_inc(pbf_ps, 1)
            pe.wait_ge(pbf_ready, 1)
            pe.wait_ge(wp_folded, NCH)
            pe.wait_ge(wc_ready, TAPS)
            pe.wait_ge(sel_cast, 1)
            pe.wait_ge(mean_ready, 1)
            with pe.Fori(0, BATCH) as b:
                attention(b)
                first_front(b * NT)
                window(b * NT, 0, first=True, ln2=False)
                window(b * NT, 1, ln2=False)
                with pe.Fori(0, NT - 1) as t:
                    for w in range(2, 2 + ITEMS):
                        window(b * NT + t, w)
                window(b * NT + (NT - 1), 2, ln1=False)
                window(b * NT + (NT - 1), 3, ln1=False, front=False)
                last_end(b * NT + (NT - 1))

        @block.scalar
        def _(act):
            def step(tile, n, first=False):
                i, s = n // NS, n % NS
                if not (first and s == 0):
                    c_copy(tile, n - 1, first=first and s < 3)
                if s == 0:
                    act.wait_ge(dt_ready, tile * ITEMS + i + 1)
                for h in range(NH):
                    if not (first and s < 2):
                        act.wait_ge(scanned, tile * (2 * STEPS) + (2 * n - 3 + h))
                    act.activation(DA[:, n % 2, h, :], DT[:, i % 2, h, :], ACT.Exp,
                                   scale=AN[:, h, s:s + 1]).then_inc(dA_ready, 1)

            def c_copy(tile, n, first=False):
                act.wait_ge(c_ready, tile * STEPS + n + 1)
                if not first:
                    act.wait_ge(g_ready, tile * STEPS + (n - 1))
                act.activation(CS[:, n % 2, :], CP[:, :], ACT.Copy).then_inc(c_copied, 1)

            def xi_copy(tile, i, h):
                act.wait_ge(xi_ready, tile * (2 * ITEMS) + 2 * i + h + 1)
                act.activation(XC[:, i % 2, h, :], FP[:, h, :], ACT.Identity, bias=CB[:, h:h + 1]).then_inc(xi_copied, 1)

            def silus(tile, i):
                act.wait_ge(xi_copied, tile * (2 * ITEMS) + 2 * i + 2)
                act.activation(XC[:, i % 2], XC[:, i % 2], ACT.Silu).then_inc(xc_ready, 1)
                act.wait_ge(z_ready, tile * ITEMS + i + 1)
                act.activation(ZS[:, i % 2], FP[:, :, :], ACT.Silu).then_inc(zs_ready, 1)
                act.preload_act_table_set(LN_EXP_SET)

            def dbc_copy(tile, i):
                act.wait_ge(dbc_ready, tile * ITEMS + i + 1)
                act.activation(BC[0:32, i % 2, :], FP[0:32, 0, :], ACT.Copy).then_inc(hi_ready, 1)
                act.activation(DTR[:, :], FP[32:32 + DT_RANK, 0, :], ACT.Copy).then_inc(dtr_ready, 1)

            def mid(tile, i):
                act.wait_ge(rest_ready, tile * ITEMS + i + 1)
                act.activation(BC[32:64, i % 2, :], R[32:64, :], ACT.Copy).then_inc(mid_ready, 1)

            def dt_abs(tile, i):
                act.wait_ge(dtp_ready, tile * ITEMS + i + 1)
                for h in range(NH):
                    act.activation(DTX[:, i % 2, h, :], FP[:, h, :], ACT.Abs, bias=DB[:, h:h + 1]).then_inc(abs_ready, 1)
                    act.activation(DT[:, i % 2, h, :], FP[:, h, :], ACT.Relu, bias=DB[:, h:h + 1]).then_inc(relu_ready, 1)

            def dt_exp(tile, i):
                act.wait_ge(abs_ready, tile * (2 * ITEMS) + 2 * i + 2)
                act.activation(DTX[:, i % 2], DTX[:, i % 2], ACT.Exp, scale=-1.0).then_inc(e_ready, 1)

            def dt_excess(tile, i):
                act.wait_ge(e_ready, tile * ITEMS + i + 1)
                act.activation(EX[:, :, :], DTX[:, i % 2], ACT.Relu, bias=NSMALL).then_inc(excess_ready, 1)

            def dt_log(tile, i):
                act.wait_ge(excess_ready, tile * ITEMS + i + 1)
                act.activation(EX[:, :, :], EX[:, :, :], ACT.Ln, bias=ONESMALL).then_inc(l_ready, 1)

            def dt_square(tile, i):
                act.wait_ge(small_ready, tile * ITEMS + i + 1)
                act.activation(DTX[:, i % 2], EM[:, :, :], ACT.Square, scale=3.0 ** -0.5).then_inc(square_ready, 1)

            def dt_large(tile, i):
                act.wait_ge(l_ready, tile * ITEMS + i + 1)
                act.activation(EX[:, :, :], EX[:, :, :], ACT.Identity, bias=NLOGSMALL).then_inc(large_ready, 1)

            def group_norm(t, d):
                for k in range(NCH):
                    last = act.activation(LV[:, k, :], X[:, k, tokens(t, d)], ACT.Identity, bias=C2[:, k:k + 1],
                                          scale=A2[:, k:k + 1])
                last.then_inc(v_ready, 1)

            def skip_term(tile, i):
                dst = SK[:, :] if i % ITEMS == 0 else YB[:, i % ITEMS, :]
                act.activation(dst, XN[:, i % ITEMS, HALO:HALO + T], ACT.Copy,
                               scale=SKIP[:, 0:1]).then_inc(skip_ready, 1)

            def square(cen, sq, v):
                act.wait_ge(cen, v)
                act.activation(LS[:, :, :], LV[:, :, :], ACT.Square).then_inc(sq, 1)

            def rstd(var, log, done, v):
                act.wait_ge(var, v)
                act.activation(RS[:, :], LP[:, :], ACT.Ln, bias=EPSC[:, 0:1]).then_inc(log, 1)
                act.wait_ge(log, v)
                act.activation(RS[:, :], RS[:, :], ACT.Exp, scale=-0.5).then_inc(done, 1)

            def window(tile, w, t, first=False, front=True, ln1=True, ln2=True):
                j = w % ITEMS
                for s in range(NS):
                    step(tile, w * NS + s, first=first)
                    if front:
                        if s == 3:
                            if not first:
                                act.wait_ge(yd_ready, tile * (2 * ITEMS) + 2 * w)
                            xi_copy(tile, w + 1, 0)
                        if s == 4:
                            xi_copy(tile, w + 1, 1)
                        if s == 5:
                            if not first:
                                act.wait_ge(yz_ready, tile * ITEMS + w)
                            silus(tile, w + 1)
                        if s == 7:
                            dbc_copy(tile, w + 1)
                        if s == 8:
                            mid(tile, w + 1)
                        if s == 9:
                            dt_abs(tile, w + 1)
                            dt_exp(tile, w + 1)
                            dt_excess(tile, w + 1)
                        if s == 10:
                            dt_log(tile, w + 1)
                            dt_square(tile, w + 1)
                        if s == 11:
                            dt_large(tile, w + 1)
                        if s == (6 if j == 2 else 14):
                            if j == 0 and ln2:
                                act.wait_ge(cen2_ready, tile + w // ITEMS)
                            skip_term(tile, w + 1)
                    if j == 0 and ln2 and s == 13:
                        square(cen2_ready, sq2_ready, tile + w // ITEMS)
                    if j == 1 and ln2 and s == 0:
                        rstd(var2_ready, log2_ready, rstd2_ready, tile + w // ITEMS)
                    if j == 2 and ln1:
                        if s == 4:
                            act.wait_ge(x1_ready, tile + w // ITEMS + 2)
                            group_norm(t, w // ITEMS + 1)
                        if s == 8:
                            square(cen1_ready, sq1_ready, tile + w // ITEMS + 2)
                        if s == 12:
                            rstd(var1_ready, log1_ready, rstd1_ready, tile + w // ITEMS + 2)

            def attention(b):
                def group_rstd(n):
                    act.wait_ge(gvar_ready, b * 2 + n)
                    act.activation(GLN[:, :], FP[:, 1, 0:NCH], ACT.Ln, bias=EPSC[:, 0:1]).then_inc(glog_ready, 1)
                    act.wait_ge(glog_ready, b * 2 + n)
                    act.activation(GRS[:, :], GLN[:, :], ACT.Exp, scale=-0.5).then_inc(grstd_ready, 1)

                act.preload_act_table_set(LN_EXP_SET)
                group_rstd(1)
                for dst, src, bias, ps, done in ((Q, bp_att, BQ, q_ps, q_ready), (K, yp_att, BK, k_ps, k_ready)):
                    act.wait_ge(ps, b + 1)
                    for o in range(NCH):
                        last = act.activation(dst[:, o, :], src[:, o, :], ACT.Identity, bias=bias[:, o:o + 1])
                    last.then_inc(done, 1)
                act.wait_ge(negmax_ready, b + 1)
                for m in range(2):
                    last = act.activation(AT[:, m, :], CP[:, m * NB:(m + 1) * NB], ACT.Exp, scale=ATT_SCALE,
                                          bias=NMX[:, m:m + 1], accum_out=RSUM[:, m:m + 1])
                last.then_inc(prob_exp, 1)
                act.wait_ge(v_ps, b + 1)
                act.activation(VS[:, :, :], FP[:, :, :], ACT.Copy).then_inc(v_ready_att, 1)
                act.wait_ge(probT_ps, b + 1)
                act.activation(ATT[:, :, :], BP[:, :, 0:NB], ACT.Copy).then_inc(probT_ready, 1)
                act.wait_ge(o_ps, b + 1)
                for o in range(NCH):
                    last = act.activation(O[:, o, :], yp_att[:, o, :], ACT.Identity, bias=BV16[:, o:o + 1])
                last.then_inc(o_ready, 1)
                group_rstd(2)

            def first_front(tile):
                act.wait_ge(x1_ready, tile + 1)
                group_norm(0, 0)
                square(cen1_ready, sq1_ready, tile + 1)
                rstd(var1_ready, log1_ready, rstd1_ready, tile + 1)
                xi_copy(tile, 0, 0)
                xi_copy(tile, 0, 1)
                silus(tile, 0)
                dbc_copy(tile, 0)
                mid(tile, 0)
                dt_abs(tile, 0)
                dt_exp(tile, 0)
                dt_excess(tile, 0)
                dt_log(tile, 0)
                dt_square(tile, 0)
                dt_large(tile, 0)
                skip_term(tile, 0)

            def last_end(tile):
                c_copy(tile, STEPS - 1)
                square(cen2_ready, sq2_ready, tile + 1)
                rstd(var2_ready, log2_ready, rstd2_ready, tile + 1)

            act.wait_ge(w_loaded, 16 * W_LOADS)
            act.preload_act_table_set(LN_EXP_SET)
            act.activation(AN[:, :, :], AN[:, :, :], ACT.Exp).then_inc(an_exp, 1)
            act.wait_ge(mean_ready, 6)
            act.activation(NLOGSMALL, ZERO, ACT.Ln, bias=ONESMALL).then_inc(logsmall_ready, 1)
            act.wait_ge(logsmall_ready, 1)
            act.activation(NLOGSMALL, NLOGSMALL, ACT.Copy, scale=-1.0).then_inc(logsmall_ready, 1)
            act.wait_ge(logsmall_ready, 2)
            act.wait_ge(an_ready, 1)
            with act.Fori(0, BATCH) as b:
                attention(b)
                first_front(b * NT)
                window(b * NT, 0, 0, first=True, ln2=False)
                window(b * NT, 1, 0, ln2=False)
                with act.Fori(0, NT - 1) as t:
                    for w in range(2, 2 + ITEMS):
                        window(b * NT + t, w, t)
                window(b * NT + (NT - 1), 2, 0, ln1=False)
                window(b * NT + (NT - 1), 3, 0, ln1=False, front=False)
                last_end(b * NT + (NT - 1))

        @block.vector
        def _(dve):
            def make_u(tile, n, first=False):
                i, s = n // NS, n % NS
                if s == 0:
                    dve.wait_ge(dtx_ready, tile * ITEMS + i + 1)
                dve.wait_ge(b_ready, tile * STEPS + n + 1)
                if not (first and s < 2):
                    dve.wait_ge(scanned, tile * (2 * STEPS) + (2 * n - 2))
                dve.tensor_tensor(U[:, n % 2], DTX[:, i % 2], BP[:, n % 2, :].unsqueeze(1).broadcast_to([P, NH, T]),
                                  ALU.mult).then_inc(u_ready, 1)

            def scan(tile, n, first=False):
                i, s = n // NS, n % NS
                dve.wait_ge(u_ready, tile * STEPS + n + 1)
                if not (first and s < 2):
                    dve.wait_ge(state_kept, tile * STEPS + (n - 1))
                for h in range(NH):
                    dve.wait_ge(dA_ready, tile * (2 * STEPS) + (2 * n + h + 1))
                    dve.tensor_tensor_scan(H[:, n % 2, h, :], DA[:, n % 2, h, :], U[:, n % 2, h, :],
                                           HS[:, i % ITEMS, h, s:s + 1], ALU.mult, ALU.add).then_inc(scanned, 1)

            def y_and_d(tile, i):
                dve.wait_ge(g_summed, tile * STEPS + NS * (i + 1))
                for h in range(NH):
                    dve.scalar_tensor_tensor(out=YZ[:, h, :], in0=XC[:, i % 2, h, :], scalar=DP[:, h:h + 1],
                                             in1=YP[:, h, :], op0=ALU.mult, op1=ALU.add).then_inc(yd_ready, 1)

            def bc_rest(tile, i):
                dve.wait_ge(hi_ready, tile * ITEMS + i + 1)
                dve.wait_ge(dtr_ready, tile * ITEMS + i + 1)
                dve.tensor_tensor(R[32:64, :], FP[0:32, 0, :], BC[0:32, i % 2, :], ALU.subtract).then_inc(rest_ready, 1)

            def bc_lo(tile, i):
                dve.wait_ge(mid_ready, tile * ITEMS + i + 1)
                dve.tensor_tensor(BC[64:96, i % 2, :], R[32:64, :], BC[32:64, i % 2, :], ALU.subtract).then_inc(lo_ready, 1)

            def add_skip(tile, i):
                dve.wait_ge(out_ready, tile * ITEMS + i + 1)
                dve.wait_ge(skip_ready, tile * ITEMS + i + 1)
                skip_part = SK[:, :] if i % ITEMS == 0 else YB[:, i % ITEMS, :]
                dve.tensor_tensor(YB[:, i % ITEMS, :], skip_part, LP[:, :], ALU.add).then_inc(yb_ready, 1)

            def dt_small(tile, i):
                dve.wait_ge(e_ready, tile * ITEMS + i + 1)
                dve.tensor_scalar(EM[:, :, :], DTX[:, i % 2], SMALL, None, ALU.min).then_inc(small_ready, 1)

            def dt_cubic(tile, i):
                dve.wait_ge(square_ready, tile * ITEMS + i + 1)
                dve.scalar_tensor_tensor(out=DTX[:, i % 2], in0=EM[:, :, :], scalar=-0.5, in1=DTX[:, i % 2],
                                         op0=ALU.mult, op1=ALU.add).then_inc(cubic_ready, 1)

            def dt_poly(tile, i):
                dve.wait_ge(cubic_ready, tile * ITEMS + i + 1)
                dve.scalar_tensor_tensor(out=DTX[:, i % 2], in0=DTX[:, i % 2], scalar=1.0, in1=EM[:, :, :],
                                         op0=ALU.add, op1=ALU.mult).then_inc(poly_ready, 1)

            def centre(src, mu, done, v):
                dve.wait_ge(mu, v)
                dve.tensor_tensor(LV[:, :, :], src[:, :, :], LP[:, :].unsqueeze(1).broadcast_to([P, NCH, T]),
                                  ALU.subtract).then_inc(done, 1)

            def scale_norm(v, first=False):
                if first:
                    dve.memset(XN[:, :, 0:HALO], 0.0).then_inc(halo_kept, 1)
                else:
                    dve.tensor_copy(XN[:, :, 0:HALO], XN[:, :, T:T + HALO]).then_inc(halo_kept, 1)
                dve.wait_ge(rstd1_ready, v)
                dve.tensor_tensor(LV[:, :, :], LV[:, :, :], RS[:, :].unsqueeze(1).broadcast_to([P, NCH, T]),
                                  ALU.mult).then_inc(scaled1, 1)

            def apply_norm(v):
                dve.wait_ge(scaled1, v)
                dve.wait_ge(halo_kept, v)
                for k in range(NCH):
                    last = dve.tensor_scalar(XN[:, k, HALO:HALO + T], LV[:, k, :], NG[:, k:k + 1], NBI[:, k:k + 1],
                                             ALU.mult, ALU.add)
                last.then_inc(xn_ready, 1)

            def finish(t, d, o, v):
                dve.wait_ge(proj_ready, v * NCH + (o + 1))
                xt = X[:, o, tokens(t, d)]
                dve.scalar_tensor_tensor(out=xt, in0=proj_bank(o), scalar=PBF[:, o:o + 1], in1=xt,
                                         op0=ALU.add, op1=ALU.add).then_inc(final_ready, 1)

            def window(tile, w, t, first=False, front=True, ln1=True, ln2=True):
                j = w % ITEMS
                for s in range(NS):
                    n = w * NS + s
                    if front or s < NS - 1:
                        make_u(tile, n + 1, first=first and n + 1 < 2)
                    scan(tile, n, first=first)
                    if s == 2 and not first:
                        y_and_d(tile, w - 1)
                    if s == 7 and front:
                        bc_rest(tile, w + 1)
                    if s == out_step(j) + 1 and not first:
                        add_skip(tile, w - 1)
                    if front:
                        if s == 8:
                            bc_lo(tile, w + 1)
                        if s == 9:
                            dt_small(tile, w + 1)
                        if s == 10:
                            dt_cubic(tile, w + 1)
                        if s == 11:
                            dt_poly(tile, w + 1)
                    if j == 0 and ln2 and s == 12:
                        centre(YB, mu2_ready, cen2_ready, tile + w // ITEMS)
                    if j == 1 and ln2:
                        for at, o in ((6, 0), (12, 1), (13, 2), (15, 3)):
                            if s == at:
                                finish(t, w // ITEMS - 1, o, tile + (w // ITEMS - 1))
                    if j == 2 and ln1:
                        if s == 7:
                            centre(LV, mu1_ready, cen1_ready, tile + w // ITEMS + 2)
                        if s == 13:
                            dve.wait_ge(skip_ready, tile * ITEMS + w + 2)
                            scale_norm(tile + w // ITEMS + 2)
                        if s == 14:
                            apply_norm(tile + w // ITEMS + 2)

            def slice_stats(slices):
                for t in slices:
                    for k in range(NCH):
                        last = dve.bn_stats(ST[:, k, t, :], X[:, k, t * T:(t + 1) * T])
                return last

            def row_sums(k, t0, t1):
                rows = T // HW
                return dve.tensor_reduce(
                    S4[:, k, t0 * rows:t1 * rows],
                    X[:, k, t0 * T:t1 * T].rearrange("p (h w q) -> p h w q", h=(t1 - t0) * rows, q=POOL), AX_X, ALU.add)

            def block_sums(k, t0, t1):
                r0, r1 = t0 * (T // HW), t1 * (T // HW)
                wide = HW // POOL
                rows = S4[:, k, r0:r1]
                dve.tensor_reduce(XS[:, k, r0 * HW // SS:r1 * HW // SS],
                                  rows.rearrange("p h (w q) -> p (h w) q", q=POOL), AX_X, ALU.add)
                return dve.tensor_reduce(
                    XA[:, k, r0 // POOL * wide:r1 // POOL * wide].rearrange("p (h w) -> p h w", w=wide),
                    rows.rearrange("p (h q) w -> p h w q", q=POOL), AX_X, ALU.add)

            def attention(b):
                def group_moments(n, mean, var, scale, shift):
                    dve.wait_ge(gmean_ready, b * 2 + n)
                    dve.tensor_tensor(DEV[:, :], mean, FP[:, 0, 0:NCH], ALU.subtract).then_inc(chain, 1)
                    link()
                    dve.tensor_tensor(GSQ[:, :], DEV[:, :], DEV[:, :], ALU.mult).then_inc(chain, 1)
                    link()
                    dve.tensor_tensor(GVAR[:, :], GSQ[:, :], var, ALU.add).then_inc(dev_ready, 1)
                    dve.wait_ge(grstd_ready, b * 2 + n)
                    dve.tensor_copy(scale, GRS[:, :]).then_inc(chain, 1)
                    link()
                    dve.scalar_tensor_tensor(out=shift, in0=FP[:, 0, 0:NCH], scalar=-1.0, in1=GRS[:, :],
                                             op0=ALU.mult, op1=ALU.mult).then_inc(gshift_ready, 1)
                    dve.wait_ge(gshift_ready, b * 2 + n)

                links = [0]

                def link():
                    links[0] += 1
                    dve.wait_ge(chain, b * CHAIN + links[0])

                dve.memset(HS[:, :, :, :], 0.0).then_inc(state_zeroed, 1)
                dve.wait_ge(x_last, b * 16 + 16)
                slice_stats((NT - 1,)).then_inc(x_stats, 1)
                for k in range(NCH):
                    if k == NCH - 1:
                        dve.wait_ge(x_stats, b + 1)
                    last = row_sums(k, NT - 1, NT)
                last.then_inc(s4_ready, 1)
                for k in range(NCH):
                    last = dve.bn_aggr(MV[:, k, :], ST[:, k].rearrange("p t n -> p (t n)"))
                last.then_inc(chain, 1)
                link()
                dve.tensor_copy(GMS[:, :], MV[:, :, 0]).then_inc(x_aggr, 1)
                dve.wait_ge(s4_ready, b + 1)
                for k in range(NCH):
                    last = block_sums(k, NT - 1, NT)
                last.then_inc(pooled, 1)
                dve.wait_ge(x_aggr, b + 1)
                group_moments(1, GMS[:, :], MV[:, :, 1], GRS16[:, :], GSH[:, :])
                dve.tensor_scalar(GRS16[:, :], GRS16[:, :], 1.0 / SS, None, ALU.mult).then_inc(chain, 1)
                dve.tensor_scalar(GSH16[:, :], GSH[:, :], float(SS), None, ALU.mult).then_inc(chain, 1)
                links[0] += 1
                link()
                dve.wait_ge(pooled, b + 1)
                for k in range(NCH):
                    dve.tensor_scalar(XSN[:, k, :], XS[:, k, :], GRS[:, k:k + 1], GSH16[:, k:k + 1], ALU.mult, ALU.add)
                    last = dve.tensor_scalar(XA[:, k, :], XA[:, k, :], GRS16[:, k:k + 1], GSH[:, k:k + 1],
                                             ALU.mult, ALU.add)
                last.then_inc(pooled_norm, 1)
                dve.wait_ge(score_ps, b + 1)
                for m in range(2):
                    last = dve.tensor_reduce(MX[:, m:m + 1], CP[:, m * NB:(m + 1) * NB], AX_X, ALU.max)
                last.then_inc(max_ready, 1)
                dve.wait_ge(max_ready, b + 1)
                dve.tensor_scalar(NMX[:, :], MX[:, :], -ATT_SCALE, None, ALU.mult).then_inc(negmax_ready, 1)
                dve.wait_ge(prob_exp, b + 1)
                dve.reciprocal(RINV[:, :], RSUM[:, :]).then_inc(rsum_inv, 1)
                dve.wait_ge(rsum_inv, b + 1)
                for m in range(2):
                    last = dve.tensor_scalar(AT[:, m, :], AT[:, m, :], RINV[:, m:m + 1], None, ALU.mult)
                last.then_inc(prob_ready, 1)
                dve.wait_ge(o_ready, b + 1)
                for k in range(NCH):
                    last = dve.bn_stats(SO[:, k, :], O[:, k, :])
                last.then_inc(o_stats, 1)
                dve.wait_ge(o_stats, b + 1)
                for k in range(NCH):
                    last = dve.tensor_scalar(XSC[:, k, :], XS[:, k, :], 1.0 / SS, MV[:, k, 0:1], ALU.mult, ALU.subtract)
                last.then_inc(xs_centred, 1)
                for k in range(NCH):
                    last = dve.bn_aggr(OV[:, k, :], SO[:, k, :])
                last.then_inc(o_aggr, 1)
                dve.wait_ge(o_aggr, b + 1)
                for k in range(NCH):
                    last = dve.tensor_scalar(OC[:, k, :], O[:, k, :], OV[:, k, 0:1], None, ALU.subtract)
                last.then_inc(o_centred, 1)
                dve.wait_ge(o_centred, b + 1)
                dve.wait_ge(xs_centred, b + 1)
                dve.tensor_tensor(OXP[:, :, :], OC[:, :, :], XSC[:, :, :], ALU.mult).then_inc(chain, 1)
                link()
                dve.tensor_reduce(COV[:, :], OXP[:, :, :], AX_X, ALU.add).then_inc(cov_ready, 1)
                dve.tensor_tensor(M1[:, :], MV[:, :, 0], OV[:, :, 0], ALU.add).then_inc(chain, 1)
                dve.wait_ge(cov_ready, b + 1)
                dve.scalar_tensor_tensor(out=V1[:, :], in0=COV[:, :], scalar=2.0 / NB, in1=MV[:, :, 1],
                                         op0=ALU.mult, op1=ALU.add).then_inc(chain, 1)
                links[0] += 1
                link()
                dve.tensor_tensor(V1[:, :], V1[:, :], OV[:, :, 1], ALU.add).then_inc(moments_ready, 1)
                dve.wait_ge(moments_ready, b + 1)
                group_moments(2, M1[:, :], V1[:, :], A2[:, :], C2[:, :])
                assert links[0] == CHAIN

            def first_front(tile, image):
                xt, ot = attention_views(0, 0)
                dve.tensor_tensor(xt, xt, ot, ALU.add).then_inc(x1_ready, 1)
                centre(LV, mu1_ready, cen1_ready, tile + 1)
                scale_norm(tile + 1, first=True)
                apply_norm(tile + 1)
                bc_rest(tile, 0)
                bc_lo(tile, 0)
                dt_small(tile, 0)
                dt_cubic(tile, 0)
                dt_poly(tile, 0)
                make_u(tile, 0, first=True)
                dve.wait_ge(state_zeroed, image + 1)

            def last_end(tile, following=None):
                more = following is not None
                if more:
                    dve.wait_ge(x_early, following * ((NT - 1) * 16) + (NT - 1) * 16)
                    slice_stats((0, 1))
                y_and_d(tile, ITEMS - 1)
                if more:
                    slice_stats((2,))
                add_skip(tile, ITEMS - 1)
                if more:
                    slice_stats((3, 4))
                centre(YB, mu2_ready, cen2_ready, tile + 1)
                if more:
                    slice_stats((5, 6))
                    dve.wait_ge(state_kept, following * (NT * STEPS))
                    for k in range(NCH - 1):
                        row_sums(k, 0, NT - 1)
                finish(0, NT - 1, 0, tile)
                if more:
                    row_sums(NCH - 1, 0, NT - 1).then_inc(s4_early, 1)
                for o in range(1, NCH):
                    finish(0, NT - 1, o, tile)
                if more:
                    dve.wait_ge(s4_early, following + 1)
                    for k in range(NCH):
                        block_sums(k, 0, NT - 1)

            dve.wait_ge(w_loaded, 16 * W_LOADS)
            dve.memset(MEAN[:, :], 1.0 / CH).then_inc(mean_ready, 1)
            dve.memset(EPSC, EPS).then_inc(mean_ready, 1)
            dve.memset(NSMALL, -SMALL).then_inc(mean_ready, 1)
            dve.memset(ONESMALL, 1.0 + SMALL).then_inc(mean_ready, 1)
            dve.memset(ZERO, 0.0).then_inc(mean_ready, 1)
            dve.tensor_scalar(BV16, BV, float(SS), None, ALU.mult).then_inc(mean_ready, 1)
            dve.tensor_copy(SEL[:, :], ring_flat[0:96, 0:2 * NS]).then_inc(sel_cast, 1)
            taps = YB[:, 1:3, :].rearrange("p a b -> p (a b)").rearrange("p (k e) -> p k e", k=TAPS)
            for k in range(TAPS):
                dve.tensor_tensor(WC[:, k, :], YB[:, 0, 0:D_INNER], taps[:, k, :], ALU.mult).then_inc(wc_ready, 1)
            dve.wait_ge(logsmall_ready, 2)
            dve.wait_ge(an_exp, 1)
            dve.tensor_scalar(AN[:, :, :], AN[:, :, :], -1.0, None, ALU.mult).then_inc(an_ready, 1)
            dve.wait_ge(pbf_ps, 1)
            dve.tensor_tensor(PBF, PB, FP[:, 0, 0:NCH], ALU.add).then_inc(pbf_ready, 1)
            for k in range(NCH):
                dve.tensor_scalar(WP[:, k, :], WP[:, k, :], NG[:, k:k + 1], None, ALU.mult).then_inc(wp_folded, 1)
            dve.wait_ge(sel_cast, 1)
            dve.wait_ge(wc_ready, TAPS)
            dve.wait_ge(pbf_ready, 1)
            dve.wait_ge(wp_folded, NCH)
            def image(b, following=None):
                attention(b)
                first_front(b * NT, b)
                window(b * NT, 0, 0, first=True, ln2=False)
                window(b * NT, 1, 0, ln2=False)
                with dve.Fori(0, NT - 1) as t:
                    for w in range(2, 2 + ITEMS):
                        window(b * NT + t, w, t)
                window(b * NT + (NT - 1), 2, NT - 1, ln1=False)
                window(b * NT + (NT - 1), 3, NT - 1, ln1=False, front=False)
                last_end(b * NT + (NT - 1), following)
                dve.wait_ge(g_summed, (b + 1) * (NT * STEPS))
                dve.wait_ge(state_kept, (b + 1) * (NT * STEPS))
                dve.wait_ge(scanned, (b + 1) * (2 * NT * STEPS))
                dve.wait_ge(final_ready, (b + 1) * (NT * NCH))

            dve.wait_ge(x_early, (NT - 1) * 16)
            slice_stats(range(NT - 1))
            for k in range(NCH):
                last = row_sums(k, 0, NT - 1)
            last.then_inc(s4_early, 1)
            dve.wait_ge(s4_early, 1)
            for k in range(NCH):
                block_sums(k, 0, NT - 1)
            with dve.Fori(0, BATCH - 1) as b:
                image(b, b + 1)
            image(BATCH - 1)

        @block.gpsimd
        def _(pool):
            def step(tile, n, first=False):
                i, s = n // NS, n % NS
                pool.wait_ge(c_copied, tile * STEPS + n + 1)
                if not (first and s < 3):
                    used = 2 if n % STEPS in (1, STEPS - 1) else 3
                    pool.wait_ge(g_summed, tile * STEPS + (n - used + 1))
                pool.wait_ge(scanned, tile * (2 * STEPS) + 2 * (n + 1))
                pool.tensor_tensor(G[:, g_slot(n)], H[:, n % 2], CS[:, n % 2, :].unsqueeze(1).broadcast_to([P, NH, T]),
                                   ALU.mult).then_inc(g_ready, 1)
                pool.tensor_copy(HS[:, i % ITEMS, :, s:s + 1], H[:, n % 2, :, T - 1:T]).then_inc(state_kept, 1)

            def gate(tile, i):
                pool.wait_ge(yd_ready, tile * (2 * ITEMS) + 2 * (i + 1))
                pool.tensor_tensor(YZ[:, :, :], YZ[:, :, :], ZS[:, i % 2], ALU.mult).then_inc(yz_ready, 1)

            def dt_first(tile, i):
                pool.wait_ge(large_ready, tile * ITEMS + i + 1)
                pool.tensor_tensor(DT[:, i % 2], DT[:, i % 2], EX[:, :, :], ALU.add).then_inc(dt_begun, 1)

            def dt_sum(tile, i):
                pool.wait_ge(dt_begun, tile * ITEMS + i + 1)
                pool.wait_ge(poly_ready, tile * ITEMS + i + 1)
                pool.tensor_tensor(DT[:, i % 2], DT[:, i % 2], DTX[:, i % 2], ALU.add).then_inc(dt_ready, 1)

            def dt_x(tile, i):
                pool.wait_ge(dt_ready, tile * ITEMS + i + 1)
                pool.tensor_tensor(DTX[:, i % 2], DT[:, i % 2], XC[:, i % 2], ALU.mult).then_inc(dtx_ready, 1)

            def normalise(v):
                pool.wait_ge(rstd2_ready, v)
                pool.tensor_tensor(LS[:, :, :], LV[:, :, :], RS[:, :].unsqueeze(1).broadcast_to([P, NCH, T]),
                                   ALU.mult).then_inc(yn_ready, 1)

            def window(tile, w, t, first=False, front=True, ln1=True, ln2=True):
                j = w % ITEMS
                for s in range(NS):
                    step(tile, w * NS + s, first=first)
                    if s == 3 and not first:
                        gate(tile, w - 1)
                    if s == 1 and j == 1 and ln2:
                        normalise(tile + w // ITEMS)
                    if s == 0 and j == 2 and ln1:
                        xt, ot = attention_views(t, w // ITEMS + 1)
                        pool.tensor_tensor(xt, xt, ot, ALU.add).then_inc(x1_ready, 1)
                    if front:
                        if s == 10:
                            dt_first(tile, w + 1)
                        if s == 11:
                            dt_sum(tile, w + 1)
                        if s == 13:
                            dt_x(tile, w + 1)

            with pool.Fori(0, BATCH) as b:
                dt_first(b * NT, 0)
                dt_sum(b * NT, 0)
                dt_x(b * NT, 0)
                window(b * NT, 0, 0, first=True)
                window(b * NT, 1, 0, ln2=False)
                with pool.Fori(0, NT - 1) as t:
                    for w in range(2, 2 + ITEMS):
                        window(b * NT + t, w, t)
                window(b * NT + (NT - 1), 2, 0, ln1=False)
                window(b * NT + (NT - 1), 3, 0, front=False)
                gate(b * NT + (NT - 1), ITEMS - 1)
                normalise(b * NT + NT)


INPUTS = {
    "x": (BATCH, CH, L), "wqkv": (3, CH, CH), "bq": (P, NCH), "bk": (P, NCH), "bv": (P, NCH), "norm_g": (P, NCH),
    "norm_b": (P, NCH), "w_in": (P, 2 * D_INNER), "conv_w": (TAPS, D_INNER), "conv_b": (P, NH),
    "w_x": (D_INNER, 2 * NS + DT_RANK), "w_dt": (DT_RANK, D_INNER), "dt_b": (P, NH), "a_log": (D_INNER, NS),
    "d_param": (P, NH), "w_out": (D_INNER, P), "w_proj": (CH, CH), "proj_b": (P, NCH), "skip": (1, 1),
    "eye": (P, P), "group_mean": (P, P), "row_select": (96, 2 * NS),
}


def kernel(**inputs):
    import numpy as np
    import concourse.bacc as bacc
    from concourse.bass_utils import run_bass_kernel_spmd

    a = {k: np.asarray(v) for k, v in inputs.items()}

    def columns(v):
        return v.reshape(-1, P).T

    x_proj = a["L1_conv_x_proj_w"]
    rows = np.arange(96)[:, None] % (2 * NS) == np.arange(2 * NS)[None, :]
    laid_out = {
        "x": a["x"].reshape(BATCH, CH, L),
        "wqkv": np.stack([a["L0_conv_Wq"].T, a["L0_conv_Wk"].T, a["L0_conv_Wv"].T]),
        "bq": columns(a["L0_conv_bq"]), "bk": columns(a["L0_conv_bk"]), "bv": columns(a["L0_conv_bv"]),
        "norm_g": columns(a["L1_conv_norm_g"]), "norm_b": columns(a["L1_conv_norm_b"]),
        "w_in": a["L1_conv_in_proj_w"].T, "conv_w": a["L1_conv_conv_w"].T, "conv_b": columns(a["L1_conv_conv_b"]),
        "w_x": np.concatenate([x_proj[DT_RANK:], x_proj[:DT_RANK]]).T,
        "w_dt": a["L1_conv_dt_proj_w"].T, "dt_b": columns(a["L1_conv_dt_proj_b"]),
        "a_log": a["L1_conv_A_log"], "d_param": columns(a["L1_conv_D_param"]), "w_out": a["L1_conv_out_proj_w"].T,
        "w_proj": a["L1_conv_proj_w"].T, "proj_b": columns(a["L1_conv_proj_b"]),
        "skip": a["L1_conv_skip_scale"].reshape(1, 1),
        "eye": np.eye(P, dtype=np.float32),
        "group_mean": np.kron(np.eye(P // GROUP, dtype=np.float32), np.full((GROUP, GROUP), 1.0 / GROUP, np.float32)),
        "row_select": rows.astype(np.float32),
    }
    nc = bacc.Bacc("TRN2", target_bir_lowering=False, num_devices=1)
    arrays, aps = {}, {}
    for name, shape in INPUTS.items():
        arrays[f"in_{name}"] = np.ascontiguousarray(laid_out[name])
        assert arrays[f"in_{name}"].shape == shape
        aps[name] = nc.dram_tensor(f"in_{name}", shape, F32, kind="ExternalInput").ap()
    out = nc.dram_tensor("out", (BATCH, CH, L), F32, kind="ExternalOutput").ap()
    block_ssm_kernel(nc, out=out, **aps)
    r = run_bass_kernel_spmd(nc, [arrays], core_ids=[0])
    return r.results[0]["out"].reshape(BATCH, CH, HW, HW)
```
